# Optimizing a Trainium2 kernel written in Bass

```python
import numpy as np
import jax
import jax.numpy as jnp

def _softmax(x, axis=-1):
    return jax.nn.softmax(x, axis=axis)

def _gelu(x):
    return jax.nn.gelu(x, approximate=True)

def _silu(x):
    return jax.nn.silu(x)

def _sigmoid(x):
    return jax.nn.sigmoid(x)

def _layernorm(x, axis=-1, eps=1e-05):
    m = jnp.mean(x, axis=axis, keepdims=True)
    v = jnp.var(x, axis=axis, keepdims=True)
    return (x - m) / jnp.sqrt(v + eps)

def _scatter_add(tgt, idx, src, axis=0):
    return tgt.at[idx].add(src)

def _segment_sum(src, seg, n):
    return jax.ops.segment_sum(src, seg, n)
kernel_name = 'mk_decoder_postln_d1_seqx_r4_b64eb7'

def setup_inputs(seed: int=0):
    np.random.seed(seed)
    _w = jnp.asarray

    def _rec_inputs():
        import jax
        import jax.numpy as jnp
        _rk = jax.random.key(seed)
        x = 7.22e-05 + 1 * jax.random.normal(jax.random.fold_in(_rk, 1), (16, 256, 256), jnp.float32)
        _lenS = 256 - jax.random.randint(jax.random.fold_in(_rk, 7), (16,), 0, max(1, 256 // 4) + 1, jnp.int32)
        _lenS2 = 256 - jax.random.randint(jax.random.fold_in(_rk, 8), (16,), 0, max(1, 256 // 4) + 1, jnp.int32)
        _ctx_1024P = jax.random.normal(jax.random.fold_in(_rk, 11), (16, 16, 256), jnp.float32)
        _ctx_1024c = jax.random.dirichlet(jax.random.fold_in(_rk, 511), 0.3 * jnp.ones((16,), jnp.float32), (16, 256))
        _ctx_1024t = jnp.einsum('bsk,bkd->bsd', _ctx_1024c, _ctx_1024P)
        _ctx_1024t = _ctx_1024t * jax.lax.rsqrt(jnp.mean(jnp.square(_ctx_1024t)) + 1e-12) * 0.953939
        ctx_1024 = 4.13588e-05 + 0.999923 * (_ctx_1024t + 0.3 * jax.random.normal(jax.random.fold_in(_rk, 611), (16, 256, 256), jnp.float32))
        return (x, ctx_1024)
    x, ctx_1024 = _rec_inputs()

    def _L0_attn_setup():
        import jax, jax.numpy as jnp
        import numpy as np
        D_MODEL = 256
        N_HEADS = 16
        HEAD_DIM = D_MODEL // N_HEADS
        WINDOW = 128
        PREFIX = 16
        B = 2
        S = 1024

        def _windowed_global_attention(q, k, v):
            Bb, H, S_, Dh = q.shape
            W, P = (WINDOW, PREFIX)
            C = S_ // W
            scale = 1.0 / np.sqrt(Dh).astype(np.float32)
            qc = q.reshape(Bb, H, C, W, Dh)
            kp = jnp.pad(k, ((0, 0), (0, 0), (W, 0), (0, 0)))
            vp = jnp.pad(v, ((0, 0), (0, 0), (W, 0), (0, 0)))
            tail_idx = jnp.arange(C)[:, None] * W + jnp.arange(2 * W)[None, :]
            kt = kp[:, :, tail_idx, :]
            vt = vp[:, :, tail_idx, :]
            kg = k[:, :, :P, :]
            vg = v[:, :, :P, :]
            sg = jnp.einsum('bhcqd,bhkd->bhcqk', qc, kg) * scale
            st = jnp.einsum('bhcqd,bhckd->bhcqk', qc, kt) * scale
            q_pos = jnp.arange(C)[:, None] * W + jnp.arange(W)[None, :]
            kt_pos = jnp.arange(C)[:, None] * W - W + jnp.arange(2 * W)[None, :]
            mg = jnp.arange(P)[None, None, :] <= q_pos[:, :, None]
            diff = q_pos[:, :, None] - kt_pos[:, None, :]
            mt = (diff >= 0) & (diff < W) & (kt_pos[:, None, :] >= P)
            neg = jnp.asarray(-1000000000.0, sg.dtype)
            scores = jnp.concatenate([jnp.where(mg[None, None], sg, neg), jnp.where(mt[None, None], st, neg)], axis=-1)
            attn = jax.nn.softmax(scores, axis=-1)
            vcat = jnp.concatenate([jnp.broadcast_to(vg[:, :, None], (Bb, H, C, P, Dh)), vt], axis=3)
            out = jnp.einsum('bhcqk,bhckd->bhcqd', attn, vcat)
            return out.reshape(Bb, H, S_, Dh)
        key = jax.random.key(seed)
        k1, k2, k3 = jax.random.split(key, 3)
        x = jax.random.normal(k1, (B, S, D_MODEL), dtype=jnp.float32)
        w_qkv = jax.random.normal(k2, (3 * D_MODEL, D_MODEL), dtype=jnp.float32) * 0.02
        w_out = jax.random.normal(k3, (D_MODEL, D_MODEL), dtype=jnp.float32) * 0.02
        return {'x': x, 'w_qkv': w_qkv, 'w_out': w_out}
    _L0_attn_all = _L0_attn_setup()
    _L0_attn_in = {k: v for k, v in _L0_attn_all.items() if k in ('w_qkv', 'w_out')}
    del _L0_attn_all

    def _L0_xattn_setup():
        import jax, jax.numpy as jnp
        import numpy as np
        import math
        N_EMBD = 256
        BLOCK_SIZE = 512
        B = 4
        key = jax.random.key(seed)
        ks = jax.random.split(key, 9)
        s = 0.02
        return {'q': jax.random.normal(ks[0], (B, BLOCK_SIZE, N_EMBD), jnp.float32), 'k': jax.random.normal(ks[1], (B, BLOCK_SIZE, N_EMBD), jnp.float32), 'v': jax.random.normal(ks[2], (B, BLOCK_SIZE, N_EMBD), jnp.float32), 'wq_w': jax.random.normal(ks[3], (N_EMBD, N_EMBD), jnp.float32) * s, 'wq_b': jax.random.normal(ks[4], (N_EMBD,), jnp.float32) * s, 'wk_w': jax.random.normal(ks[5], (N_EMBD, N_EMBD), jnp.float32) * s, 'wk_b': jax.random.normal(ks[6], (N_EMBD,), jnp.float32) * s, 'wv_w': jax.random.normal(ks[7], (N_EMBD, N_EMBD), jnp.float32) * s, 'wv_b': jax.random.normal(ks[8], (N_EMBD,), jnp.float32) * s, 'causal': 1}
    _L0_xattn_all = _L0_xattn_setup()
    _L0_xattn_in = {k: v for k, v in _L0_xattn_all.items() if k in ('wq_w', 'wq_b', 'wk_w', 'wk_b', 'wv_w', 'wv_b')}
    del _L0_xattn_all

    def _L0_ffn_setup():
        import jax, jax.numpy as jnp
        import numpy as np
        B, T, D, E, H = (4, 512, 256, 4, 8)
        EPS = 1e-05

        def _uniform(k, shape, bound):
            return jax.random.uniform(k, shape, jnp.float32, -bound, bound)

        def _layernorm(x, w, b):
            mu = jnp.mean(x, axis=-1, keepdims=True)
            var = jnp.mean(jnp.square(x - mu), axis=-1, keepdims=True)
            return (x - mu) * jax.lax.rsqrt(var + EPS) * w + b
        key = jax.random.key(seed)
        ks = jax.random.split(key, 12)
        wb = np.sqrt(6.0 / D) / np.sqrt(6.0)
        wb = 1.0 / np.sqrt(D)
        return {'x': jax.random.normal(ks[0], (B, T, D), jnp.float32), 'router_prob': jax.random.uniform(ks[1], (B, T, E), jnp.float32), 'norm_w': jnp.ones((D,), jnp.float32), 'norm_b': jnp.zeros((D,), jnp.float32), 'q_w': _uniform(ks[2], (D, D), wb), 'q_b': _uniform(ks[3], (D,), wb), 'k_w': _uniform(ks[4], (D, D), wb), 'k_b': _uniform(ks[5], (D,), wb), 'v_w': _uniform(ks[6], (D, D), wb), 'v_b': _uniform(ks[7], (D,), wb), 'o_w': _uniform(ks[8], (D, D), wb), 'o_b': _uniform(ks[9], (D,), wb)}
    _L0_ffn_all = _L0_ffn_setup()
    _L0_ffn_in = {k: v for k, v in _L0_ffn_all.items() if k in ('router_prob', 'norm_w', 'norm_b', 'q_w', 'q_b', 'k_w', 'k_b', 'v_w', 'v_b', 'o_w', 'o_b')}
    del _L0_ffn_all
    return {'x': x, 'ctx_1024': ctx_1024, 'L0_attn_w_qkv': _L0_attn_in['w_qkv'], 'L0_attn_w_out': _L0_attn_in['w_out'], 'L0_xattn_wq_w': _L0_xattn_in['wq_w'], 'L0_xattn_wq_b': _L0_xattn_in['wq_b'], 'L0_xattn_wk_w': _L0_xattn_in['wk_w'], 'L0_xattn_wk_b': _L0_xattn_in['wk_b'], 'L0_xattn_wv_w': _L0_xattn_in['wv_w'], 'L0_xattn_wv_b': _L0_xattn_in['wv_b'], 'L0_ffn_router_prob': _L0_ffn_in['router_prob'], 'L0_ffn_norm_w': _L0_ffn_in['norm_w'], 'L0_ffn_norm_b': _L0_ffn_in['norm_b'], 'L0_ffn_q_w': _L0_ffn_in['q_w'], 'L0_ffn_q_b': _L0_ffn_in['q_b'], 'L0_ffn_k_w': _L0_ffn_in['k_w'], 'L0_ffn_k_b': _L0_ffn_in['k_b'], 'L0_ffn_v_w': _L0_ffn_in['v_w'], 'L0_ffn_v_b': _L0_ffn_in['v_b'], 'L0_ffn_o_w': _L0_ffn_in['o_w'], 'L0_ffn_o_b': _L0_ffn_in['o_b']}

def reference(x, ctx_1024, L0_attn_w_qkv, L0_attn_w_out, L0_xattn_wq_w, L0_xattn_wq_b, L0_xattn_wk_w, L0_xattn_wk_b, L0_xattn_wv_w, L0_xattn_wv_b, L0_ffn_router_prob, L0_ffn_norm_w, L0_ffn_norm_b, L0_ffn_q_w, L0_ffn_q_b, L0_ffn_k_w, L0_ffn_k_b, L0_ffn_v_w, L0_ffn_v_b, L0_ffn_o_w, L0_ffn_o_b):
    import jax
    import jax.numpy as jnp

    def _L0_attn_ref(x, w_qkv, w_out):
        import jax, jax.numpy as jnp
        import numpy as np
        D_MODEL = 256
        N_HEADS = 16
        HEAD_DIM = D_MODEL // N_HEADS
        WINDOW = 128
        PREFIX = 16
        B = 2
        S = 1024

        def _windowed_global_attention(q, k, v):
            Bb, H, S_, Dh = q.shape
            W, P = (WINDOW, PREFIX)
            C = S_ // W
            scale = 1.0 / np.sqrt(Dh).astype(np.float32)
            qc = q.reshape(Bb, H, C, W, Dh)
            kp = jnp.pad(k, ((0, 0), (0, 0), (W, 0), (0, 0)))
            vp = jnp.pad(v, ((0, 0), (0, 0), (W, 0), (0, 0)))
            tail_idx = jnp.arange(C)[:, None] * W + jnp.arange(2 * W)[None, :]
            kt = kp[:, :, tail_idx, :]
            vt = vp[:, :, tail_idx, :]
            kg = k[:, :, :P, :]
            vg = v[:, :, :P, :]
            sg = jnp.einsum('bhcqd,bhkd->bhcqk', qc, kg) * scale
            st = jnp.einsum('bhcqd,bhckd->bhcqk', qc, kt) * scale
            q_pos = jnp.arange(C)[:, None] * W + jnp.arange(W)[None, :]
            kt_pos = jnp.arange(C)[:, None] * W - W + jnp.arange(2 * W)[None, :]
            mg = jnp.arange(P)[None, None, :] <= q_pos[:, :, None]
            diff = q_pos[:, :, None] - kt_pos[:, None, :]
            mt = (diff >= 0) & (diff < W) & (kt_pos[:, None, :] >= P)
            neg = jnp.asarray(-1000000000.0, sg.dtype)
            scores = jnp.concatenate([jnp.where(mg[None, None], sg, neg), jnp.where(mt[None, None], st, neg)], axis=-1)
            attn = jax.nn.softmax(scores, axis=-1)
            vcat = jnp.concatenate([jnp.broadcast_to(vg[:, :, None], (Bb, H, C, P, Dh)), vt], axis=3)
            out = jnp.einsum('bhcqk,bhckd->bhcqd', attn, vcat)
            return out.reshape(Bb, H, S_, Dh)
        Bb, S_, Dm = x.shape
        qkv = x @ w_qkv.T
        q, k, v = jnp.split(qkv, 3, axis=-1)

        def heads(t):
            return t.reshape(Bb, S_, N_HEADS, HEAD_DIM).transpose(0, 2, 1, 3)
        q, k, v = (heads(q), heads(k), heads(v))
        o = _windowed_global_attention(q, k, v)
        o = o.transpose(0, 2, 1, 3).reshape(Bb, S_, Dm)
        return o @ w_out.T

    def _L0_xattn_ref(q, k, v, wq_w, wq_b, wk_w, wk_b, wv_w, wv_b, causal):
        import jax, jax.numpy as jnp
        import numpy as np
        import math
        N_EMBD = 256
        BLOCK_SIZE = 512
        B = 4
        qp = jnp.einsum('bte,oe->bto', q, wq_w) + wq_b
        kp = jnp.einsum('bte,oe->bto', k, wk_w) + wk_b
        vp = jnp.einsum('bte,oe->bto', v, wv_w) + wv_b
        scale = 1.0 / math.sqrt(N_EMBD)
        weights = jnp.einsum('bqe,bke->bqk', qp, kp) * scale
        if causal:
            T1, T2 = (qp.shape[1], kp.shape[1])
            mask = jnp.tril(jnp.ones((T1, T2), dtype=bool))
            weights = jnp.where(mask, weights, -jnp.inf)
        attn = jax.nn.softmax(weights, axis=-1)
        return jnp.einsum('bqk,bke->bqe', attn, vp)

    def _L0_ffn_ref(x, router_prob, norm_w, norm_b, q_w, q_b, k_w, k_b, v_w, v_b, o_w, o_b):
        import jax, jax.numpy as jnp
        import numpy as np
        B, T, D, E, H = (4, 512, 256, 4, 8)
        EPS = 1e-05

        def _uniform(k, shape, bound):
            return jax.random.uniform(k, shape, jnp.float32, -bound, bound)

        def _layernorm(x, w, b):
            mu = jnp.mean(x, axis=-1, keepdims=True)
            var = jnp.mean(jnp.square(x - mu), axis=-1, keepdims=True)
            return (x - mu) * jax.lax.rsqrt(var + EPS) * w + b
        e_cnt = router_prob.shape[2]
        b, t, d = x.shape
        n = t // e_cnt
        h = H
        scale = d ** (-0.5)
        qs, ks_, vs = ([], [], [])
        for e in range(e_cnt):
            xe = x[:, e * n:(e + 1) * n, :]
            xn = _layernorm(xe, norm_w, norm_b)
            m = d // 2 ** e
            xm = xn[..., :m]
            qs.append(jnp.einsum('bnm,dm->bnd', xm, q_w[:, :m]) + q_b)
            ks_.append(jnp.einsum('bnm,dm->bnd', xm, k_w[:, :m]) + k_b)
            vs.append(jnp.einsum('bnm,dm->bnd', xm, v_w[:, :m]) + v_b)
        q = jnp.concatenate(qs, axis=1)
        k = jnp.concatenate(ks_, axis=1)
        v = jnp.concatenate(vs, axis=1)
        dh = d // h
        q = q.reshape(b, t, h, dh).transpose(0, 2, 1, 3)
        k = k.reshape(b, t, h, dh).transpose(0, 2, 1, 3)
        v = v.reshape(b, t, h, dh).transpose(0, 2, 1, 3)
        attn = jnp.einsum('bhqd,bhkd->bhqk', q, k) * scale
        attn = jax.nn.softmax(attn, axis=-1)
        attn_out = jnp.einsum('bhqk,bhkd->bhqd', attn, v)
        attn_out = attn_out.transpose(0, 2, 1, 3).reshape(b, t, d)
        outs = []
        for e in range(e_cnt):
            sl = slice(e * n, (e + 1) * n)
            m = d // 2 ** e
            xm = attn_out[:, sl, :m]
            out = jnp.einsum('bnm,om->bno', xm, o_w[:m, :m]) + o_b[:m]
            pad = d - m
            if pad:
                out = jnp.pad(out, ((0, 0), (0, 0), (0, pad)))
            outs.append(out + x[:, sl, :])
        return jnp.concatenate(outs, axis=1)
    x = _layernorm(x + _L0_attn_ref(x, L0_attn_w_qkv, L0_attn_w_out), axis=-1)
    x = _layernorm(x + _L0_xattn_ref(x, ctx_1024, ctx_1024, L0_xattn_wq_w, L0_xattn_wq_b, L0_xattn_wk_w, L0_xattn_wk_b, L0_xattn_wv_w, L0_xattn_wv_b, 1), axis=-1)
    x = _layernorm(x + _L0_ffn_ref(x, L0_ffn_router_prob, L0_ffn_norm_w, L0_ffn_norm_b, L0_ffn_q_w, L0_ffn_q_b, L0_ffn_k_w, L0_ffn_k_b, L0_ffn_v_w, L0_ffn_v_b, L0_ffn_o_w, L0_ffn_o_b), axis=-1)
    return x

_drawn_inputs = setup_inputs


def setup_inputs(seed=0):
    import zlib

    import numpy as np

    out = dict(_drawn_inputs(seed))
    spreads = {'L0_ffn_norm_w': (1.0, 0.6), 'L0_ffn_norm_b': (0.0, 0.8)}
    factors = {'L0_attn_w_qkv': 3.501,
     'L0_attn_w_out': 3.472,
     'L0_xattn_wq_w': 8.0,
     'L0_xattn_wq_b': 8.0,
     'L0_xattn_wk_w': 8.0,
     'L0_xattn_wk_b': 8.0,
     'L0_xattn_wv_b': 2.997,
     'L0_ffn_q_w': 8.0,
     'L0_ffn_q_b': 8.0,
     'L0_ffn_k_w': 8.0,
     'L0_ffn_k_b': 8.0,
     'L0_ffn_v_w': 4.743,
     'L0_ffn_v_b': 8.0,
     'L0_ffn_o_w': 4.391,
     'L0_ffn_o_b': 4.398}
    for name, (base, spread) in spreads.items():
        noise = np.random.default_rng([zlib.crc32(name.encode()), seed]).standard_normal(out[name].shape)
        drawn = base * np.exp(spread * noise) if base else spread * noise
        out[name] = jnp.asarray(drawn.astype(out[name].dtype))
    for name, factor in factors.items():
        out[name] = (out[name] * factor).astype(out[name].dtype)
    return out
```

```python
from contextlib import ExitStack

import concourse.bass as bass
from concourse import mybir

F32 = mybir.dt.float32
BF16 = mybir.dt.bfloat16
ALU = mybir.AluOpType
ACT = mybir.ActivationFunctionType
AX = mybir.AxisListType

NB, S, D = 16, 256, 256
P = 128
H1, D1 = 16, D // 16
H3, D3 = 8, D // 8
PREFIX = 16
EPS = 1e-5
NEG = -1.0e30

Q1_PARTS, K1_PARTS = (0, 0, 1, 1, 0, 2), (0, 1, 0, 1, 2, 0)
Q3_PARTS, K3_PARTS = ((0, 0, 1), (1, 0, 2)), ((0, 1, 0), (1, 2, 0))
MROW = 96

NESTED = ((128, 0, 0, 128), (64, 0, 128, 192), (32, 0, 192, 256), (128, 1, 0, 64))
NESTED_OUT = ((0, 128, 0, 0, 128), (0, 64, 0, 128, 256), (0, 64, 1, 0, 64), (64, 128, 1, 0, 32))
Q3_USED = (256, 192, 128, 128, 64, 64, 64, 64)
T3_BANKS = (((0, 0), (1, 256), (4, 448)), ((2, 0), (3, 128), (5, 256), (6, 320), (7, 384)))
T3_COLS = (512, 448)

LAG = {"P": 0, "A": 1, "B": 2, "C": 3}

CONST_COLS = {}
_at = 0
for _name, _n in (("ident", 128), ("mask_q0", 512), ("mask_q1", 512), ("mask_k0", 512),
                  ("mask_k1", 512), ("ones", 64), ("pick1", H1 * S), ("pick3", H3 * S)):
    CONST_COLS[_name] = (_at, _at + _n)
    _at += _n
CONST_W = _at


def build(nc, xT, x, ctxT, consts, w1_qkvT, w1_oT, w2_qT, w2_kT, w2_vT, b2, bv2, w3_qT, w3_kT, w3_vT,
          w3_oT, b3, bv3, bo3, out):
    with ExitStack() as ctx:
        def sb(name, shape, dt=F32):
            return ctx.enter_context(nc.sbuf_tensor(name, shape, dt))

        def psum(name, shape):
            return ctx.enter_context(nc.psum_tensor(name, shape, F32))

        def sem(name):
            return ctx.enter_context(nc.semaphore(name))

        parts1_dram = nc.dram_tensor("parts1_dram", [6, D, S], BF16, kind="Internal").ap()
        parts3_dram = nc.dram_tensor("parts3_dram", [6, D, S], BF16, kind="Internal").ap()

        W1 = sb("W1", [P, 2, 3 * D])
        W1o = sb("W1o", [P, 2, D])
        W2q, W2k, W2v = sb("W2q", [P, 2, D]), sb("W2k", [P, 2, D]), sb("W2v", [P, 2, D])
        W3q, W3k, W3v, W3o = (sb(n, [P, 2, D]) for n in ("W3q", "W3k", "W3v", "W3o"))
        B2 = sb("B2", [P, 2, 2])
        B2v = sb("B2v", [P, D])
        B3 = sb("B3", [P, 4, 2])
        B3v = sb("B3v", [P, D])
        B3o = sb("B3o", [P, 2, D])
        CST = sb("CST", [P, CONST_W])
        ident = CST[:, CONST_COLS["ident"][0]:CONST_COLS["ident"][1]]
        identb = sb("identb", [P, P], BF16)
        masks = {n: sb(n, [P, 512], BF16) for n in ("mask_q0", "mask_q1", "mask_k0", "mask_k1")}
        ones_lo = CST[:, CONST_COLS["ones"][0]:CONST_COLS["ones"][0] + 32]
        ones_hi = CST[:, CONST_COLS["ones"][0] + 32:CONST_COLS["ones"][1]]
        ones32 = sb("ones32", [P, 32])
        minus_half = sb("minus_half", [P, 2])

        XT = sb("XT", [P, 2, S])
        XR = sb("XR", [P, 2, D])
        parts1 = sb("parts1", [P, 2, 3, 2, S], BF16)
        rest1 = sb("rest1", [P, 2, 2 * S])
        V1 = sb("V1", [P, 2, H1, 32])
        Q1, K1 = sb("Q1", [P, H1, S], BF16), sb("K1", [P, H1, S], BF16)
        nmax1 = sb("nmax1", [P, 2, H1])
        nmaxp1 = sb("nmaxp1", [P, 2, 32], BF16)
        mrow1 = sb("mrow1", [P, S], BF16)
        PT1 = sb("PT1", [P, 2, 3, 512])
        rsum1 = sb("rsum1", [P, 2, S])
        OT1 = sb("OT1", [P, 2, S])
        Y1, X1 = sb("Y1", [P, 2, D]), sb("X1", [P, 2, D])
        CT = sb("CT", [P, 2, S])
        X1T, Q2, K2 = sb("X1T", [P, 2, S]), sb("Q2", [P, 2, S]), sb("K2", [P, 2, S])
        V2 = sb("V2", [P, 2, D])
        nmax2, bias2 = sb("nmax2", [P, 2]), sb("bias2", [P, 2])
        sum2, rsum2 = sb("sum2", [P, 2]), sb("rsum2", [P, 2])
        P2, PT2 = sb("P2", [P, 3, P]), sb("PT2", [P, 3, P])
        Y2, X2, Z2 = sb("Y2", [P, 2, D]), sb("X2", [P, 2, D]), sb("Z2", [P, 2, D])
        XN = sb("XN", [P, 2, S])
        parts3 = sb("parts3", [P, 2, 3, 2, S], BF16)
        rest3 = sb("rest3", [P, 2, 2 * S])
        V3 = sb("V3", [P, 2, D])
        Q3, K3 = sb("Q3", [P, 2, H3, S], BF16), sb("K3", [P, 2, H3, S], BF16)
        nmax3 = sb("nmax3", [P, 2, H3])
        nmaxp3 = sb("nmaxp3", [P, 2, 32], BF16)
        mrow3 = sb("mrow3", [P, S], BF16)
        PT3 = sb("PT3", [P, 2, 2, 512])
        rsum3 = sb("rsum3", [P, 2, S])
        OT3 = sb("OT3", [P, 2, S])
        Y3, OUT = sb("Y3", [P, 2, D]), sb("OUT", [P, 2, D])
        stats = sb("stats", [P, 4, 2, 6])
        mv = sb("mv", [P, 4, 2, 2])
        vare = sb("vare", [P, 4, 2])
        rstd = sb("rstd", [P, 4, 2])
        fence = sb("fence", [P, 1])

        row_ps = psum("row_ps", [P, 2, 512])
        col_ps = psum("col_ps", [P, 2, 512])
        o_ps = psum("o_ps", [P, 512])
        sum_ps = psum("sum_ps", [P, 512])
        misc = psum("misc", [P, 2, 512])

        weights_in = sem("weights_in")
        xT_in, x_in, ctxT_in = sem("xT_in"), sem("x_in"), sem("ctxT_in")
        parts1_out, parts3_out = sem("parts1_out"), sem("parts3_out")
        stacks1_in, stacks3_in = sem("stacks1_in"), sem("stacks3_in")
        out_stored = sem("out_stored")
        const_ready, pool_ready = sem("const_ready"), sem("pool_ready")
        proj1, scores1, mrows1, scoresT1, pv1, attn1 = (
            sem(n) for n in ("proj1", "scores1", "mrows1", "scoresT1", "pv1", "attn1"))
        proj2, attn2 = sem("proj2"), sem("attn2")
        proj3, scores3, mrows3, scoresT3, pv3, attn3 = (
            sem(n) for n in ("proj3", "scores3", "mrows3", "scoresT3", "pv3", "attn3"))
        high1, mid1, exp1 = sem("high1"), sem("mid1"), sem("exp1")
        act2, pT2 = sem("act2"), sem("pT2")
        high3, mid3, exp3 = sem("high3"), sem("mid3"), sem("exp3")
        low1, low3 = sem("low1"), sem("low3")
        rstd_ready = [sem(f"rstd_ready{i}") for i in range(4)]
        evac1, max1, msplit1, mcopy1, norm1, ln1 = (
            sem(n) for n in ("evac1", "max1", "msplit1", "mcopy1", "norm1", "ln1"))
        vev2, vev2b, max2, ln2, ln2b = sem("vev2"), sem("vev2b"), sem("max2"), sem("ln2"), sem("ln2b")
        evac3, max3, msplit3, mcopy3, norm3, ln3 = (
            sem(n) for n in ("evac3", "max3", "msplit3", "mcopy3", "norm3", "ln3"))

        N_EV1, N_EV3, N_ACT2, N_LN1, N_LN2, N_LN2B, N_LN3 = 4, 10, 7, 9, 9, 7, 11
        N_SC1, N_SC3, N_T1, N_T3 = 12, 5, 12, 4

        MISC = [("C", evac3, N_EV3, 5), ("C", evac3, N_EV3, 7), ("C", evac3, N_EV3, 9), ("C", evac3, N_EV3, 10),
                ("B", act2, N_ACT2, 1), ("B", act2, N_ACT2, 3), ("B", vev2, 1, 1), ("B", act2, N_ACT2, 5),
                ("B", act2, N_ACT2, 7),
                ("A", mcopy1, 2, 1),
                ("B", pT2, 1, 1), ("B", ln2, N_LN2, 2),
                ("P", evac1, N_EV1, 1), ("P", evac1, N_EV1, 2), ("P", evac1, N_EV1, 4),
                ("C", mcopy3, 2, 1),
                ("A", ln1, N_LN1, 2),
                ("C", ln3, N_LN3, 4)]
        C1_FILL, B1_FILL, A3_FILL, B3_FILL, P_FILL, C3_FILL, A4_FILL, C4_FILL = 0, 4, 9, 10, 12, 15, 16, 17

        def fixed(t):
            return type(t) is int

        def on(stage, t):
            return not fixed(t) or 0 <= t - LAG[stage] < NB

        def wait(eng, s, n):
            if not fixed(n) or n > 0:
                eng.wait_ge(s, n)

        def misc_free(pe, t, n):
            stage, s, per, after = MISC[n - 2]
            seq = t - LAG[stage] - (1 if n < 2 else 0)
            if not fixed(t):
                pe.wait_ge(s, seq * per + after)
                return
            for m, (stage, s, per, after) in enumerate(MISC):
                if m % 2 == n % 2:
                    seq = min(t - LAG[stage] - (0 if m < n else 1), NB - 1)
                    if seq >= 0:
                        pe.wait_ge(s, seq * per + after)
            return

        def steps(eng, run):
            for t in range(4):
                run(t)
            with eng.Fori(4, NB) as t:
                run(t)
            for t in range(NB, NB + LAG["C"]):
                run(t)

        block = ctx.enter_context(nc.Block())

        @block.sync
        def _(sp):
            n = 0

            def load(dst, src):
                sp.dma_start(dst, src).then_inc(weights_in, 16)

            load(W1[:], w1_qkvT.rearrange("(k p) o -> p k o", p=P))
            load(CST[:], consts)
            for dst, src in ((W1o, w1_oT), (W2q, w2_qT), (W2k, w2_kT), (W2v, w2_vT),
                             (W3q, w3_qT), (W3k, w3_kT), (W3v, w3_vT), (W3o, w3_oT)):
                load(dst[:], src.rearrange("(k p) o -> p k o", p=P))
            load(B2[:], b2)
            load(B3[:], b3)
            load(B2v[:], bv2.partition_broadcast(P))
            load(B3v[:], bv3.partition_broadcast(P))
            sp.wait_ge(pool_ready, 1)
            for r0, r1, tile, f0, f1 in NESTED_OUT:
                load(B3o[r0:r1, tile, f0:f1], bo3[f0:f1].partition_broadcast(r1 - r0))

            def run(t):
                p, a, b, c = (t - LAG[x] for x in "PABC")

                def count(n):
                    return n if fixed(n) else sp.snap(n)

                xt_at, ct_at, xr_at, out_at = count(p * S), count(b * S), count(a * 2), count(c * 2)
                xt_free, ct_free, xr_free = count(3 * p), count(5 * b), count((a - 1) * N_LN1 + 2)
                two_c, two_p, high_c = count(2 * c + 2), count(2 * p + 2), count(4 * c + 4)
                wrote3, wrote1 = count(16 * c + 16), count(16 * p + 16)
                used3, used1 = count(c), count(N_T1 * p)
                normed = count(N_LN3 * c + N_LN3)
                if on("P", t):
                    wait(sp, proj1, xt_free)
                    sp.dma_start(XT[:], xT[:, :, bass.ds(xt_at, S)]).then_inc(xT_in, 16)
                if on("B", t):
                    wait(sp, proj2, ct_free)
                    sp.dma_start(CT[:], ctxT[:, :, bass.ds(ct_at, S)]).then_inc(ctxT_in, 16)
                if on("A", t):
                    wait(sp, ln1, xr_free)
                    sp.dma_start(XR[:], x[:, bass.ds(xr_at, 2), :]).then_inc(x_in, 16)
                if on("C", t):
                    wait(sp, pv3, used3)
                    sp.wait_ge(high3, high_c)
                    sp.wait_ge(mid3, two_c)
                    sp.wait_ge(low3, two_c)
                    sp.dma_start(parts3_dram.rearrange("s (m p) t -> p s m t", p=P),
                                 parts3[:].rearrange("p q r m t -> p (q r) m t")).then_inc(parts3_out, 16)
                    sp.wait_ge(parts3_out, wrote3)
                    for j in range(2):
                        for r in range(3):
                            rows = slice(D3 * r, D3 * r + D3)
                            sp.dma_start(Q3[rows, j, :, :], parts3_dram[Q3_PARTS[j][r]].rearrange(
                                "(h d) t -> d h t", d=D3)).then_inc(stacks3_in, 16)
                            sp.dma_start(K3[rows, j, :, :], parts3_dram[3 + K3_PARTS[j][r]].rearrange(
                                "(h d) t -> d h t", d=D3)).then_inc(stacks3_in, 16)
                if on("P", t):
                    wait(sp, scoresT1, used1)
                    sp.wait_ge(high1, two_p)
                    sp.wait_ge(mid1, two_p)
                    sp.wait_ge(low1, two_p)
                    sp.dma_start(parts1_dram.rearrange("s (m p) t -> p s m t", p=P),
                                 parts1[:].rearrange("p q r m t -> p (q r) m t")).then_inc(parts1_out, 16)
                    sp.wait_ge(parts1_out, wrote1)
                    for r in range(6):
                        rows = slice(D1 * r, D1 * r + D1)
                        sp.dma_start(Q1[rows, :, :], parts1_dram[Q1_PARTS[r]].rearrange(
                            "(h d) t -> d h t", d=D1)).then_inc(stacks1_in, 16)
                        sp.dma_start(K1[rows, :, :], parts1_dram[3 + K1_PARTS[r]].rearrange(
                            "(h d) t -> d h t", d=D1)).then_inc(stacks1_in, 16)
                if on("C", t):
                    sp.wait_ge(ln3, normed)
                    sp.dma_start(out[:, bass.ds(out_at, 2), :], OUT[:]).then_inc(out_stored, 16)

            steps(sp, run)
            sp.wait_ge(out_stored, 16 * NB)

        @block.gpsimd
        def _(pool):
            nc.gpsimd.memset(B3o[:], 0.0).then_inc(pool_ready, 1)
            for zeroed in (V1, XN, OT3, nmax3, nmaxp3):
                nc.gpsimd.memset(zeroed[:], 0.0).then_inc(pool_ready, 1)
            nc.gpsimd.memset(ones32[:], 1.0).then_inc(pool_ready, 1)
            nc.gpsimd.memset(minus_half[:], -0.5).then_inc(pool_ready, 1)
            pool.wait_ge(pool_ready, 8)

            def low_part(rest, parts, high, mid, low, i, n):
                pool.wait_ge(mid, n)
                nc.gpsimd.tensor_tensor(parts[:, i, 2, :, :].rearrange("p m t -> p (m t)"), rest[:, i, :],
                                        parts[:, i, 1, :, :].rearrange("p m t -> p (m t)"),
                                        ALU.subtract).then_inc(low, 1)

            def root(i, ready, n):
                pool.wait_ge(ready, n)
                nc.gpsimd.tensor_tensor(rstd[:, i, :], vare[:, i, :], minus_half[:], ALU.pow)\
                    .then_inc(rstd_ready[i], 1)

            def run(t):
                if on("C", t):
                    c = t - LAG["C"]
                    for i in range(2):
                        low_part(rest3, parts3, high3, mid3, low3, i, 2 * c + i + 1)
                if on("B", t):
                    b = t - LAG["B"]
                    root(1, ln2, N_LN2 * b + 7)
                    root(2, ln2b, N_LN2B * b + 5)
                if on("P", t):
                    for i in range(2):
                        low_part(rest1, parts1, high1, mid1, low1, i, 2 * t + i + 1)
                if on("A", t):
                    root(0, ln1, N_LN1 * (t - LAG["A"]) + 7)
                if on("C", t):
                    root(3, ln3, N_LN3 * (t - LAG["C"]) + 9)

            steps(pool, run)

        @block.scalar
        def _(act):
            act.wait_ge(weights_in, 16 * 18)

            def mid_part(rest, parts, evac, n, mid, i):
                act.wait_ge(evac, n)
                nc.scalar.activation(parts[:, i, 1, :, :].rearrange("p m t -> p (m t)"), rest[:, i, :],
                                     ACT.Copy).then_inc(mid, 1)

            def run(t):
                if on("C", t):
                    c = t - LAG["C"]
                    for i in range(2):
                        act.wait_ge(proj3, 4 * c + 2 + i)
                        for m in range(2):
                            nc.scalar.activation(parts3[:, i, 0, m, :], misc[:, (C1_FILL + 1 + i) % 2, m * S:m * S + S],
                                                 ACT.Identity, bias=B3[:, 2 + i, m:m + 1]).then_inc(high3, 1)
                    for i in range(2):
                        mid_part(rest3, parts3, evac3, N_EV3 * c + 7 + 2 * i, mid3, i)
                if on("B", t):
                    b = t - LAG["B"]
                    act.wait_ge(proj2, 5 * b + 1)
                    nc.scalar.activation(X1T[:].rearrange("p m t -> p (m t)"), misc[:, B1_FILL % 2, :],
                                         ACT.Copy).then_inc(act2, 1)
                    for dst, i, fill in ((K2, 1, 1), (Q2, 0, 3)):
                        act.wait_ge(proj2, 5 * b + fill + 1)
                        for m in range(2):
                            nc.scalar.activation(dst[:, m, :], misc[:, (B1_FILL + fill) % 2, m * S:m * S + S],
                                                 ACT.Identity, bias=B2[:, i, m:m + 1]).then_inc(act2, 1)
                    act.wait_ge(max2, 3 * b + 3)
                    for q, (lo, hi) in enumerate(((0, 128), (128, 384))):
                        nc.scalar.activation(P2[:].rearrange("p c k -> p (c k)")[:, lo:hi],
                                             misc[:, (B1_FILL + 4) % 2, lo:hi], ACT.Exp,
                                             bias=bias2[:, q:q + 1], scale=1.0 / 16.0,
                                             accum_out=sum2[:, q:q + 1]).then_inc(act2, 1)
                if on("A", t):
                    a = t - LAG["A"]
                    for j in range(N_T1):
                        act.wait_ge(scoresT1, N_T1 * a + j + 1)
                        if j % 3 == 0:
                            g = j // 3
                            if g >= 2:
                                act.wait_ge(pv1, 4 * a + g - 1)
                            else:
                                wait(act, pv1, 4 * a - 2 + g + 1 if not fixed(a) or a > 0 else 0)
                        nc.scalar.activation(PT1[:, (j // 3) % 2, j % 3, :], col_ps[:, j % 2, :], ACT.Exp,
                                             scale=0.25).then_inc(exp1, 1)
                if on("B", t):
                    b = t - LAG["B"]
                    act.wait_ge(attn2, 2 * b + 1)
                    nc.scalar.activation(PT2[:].rearrange("p c k -> p (c k)"), misc[:, B3_FILL % 2, 0:384],
                                         ACT.Copy).then_inc(pT2, 1)
                if on("P", t):
                    for i in range(2):
                        act.wait_ge(proj1, 3 * t + 1 + i)
                        nc.scalar.activation(parts1[:, i, 0, :, :].rearrange("p m t -> p (m t)"),
                                             misc[:, (P_FILL + i) % 2, :], ACT.Copy).then_inc(high1, 1)
                    for i in range(2):
                        mid_part(rest1, parts1, evac1, N_EV1 * t + 1 + i, mid1, i)
                if on("C", t):
                    c = t - LAG["C"]
                    wait(act, pv3, c)
                    for j in range(N_T3):
                        act.wait_ge(scoresT3, N_T3 * c + j + 1)
                        n = T3_COLS[j % 2]
                        nc.scalar.activation(PT3[:, j // 2, j % 2, 0:n], col_ps[:, j % 2, 0:n], ACT.Exp,
                                             scale=1.0 / 16.0).then_inc(exp3, 1)

            steps(act, run)

        @block.vector
        def _(dve):
            dve.wait_ge(weights_in, 16 * 18)
            dve.wait_ge(pool_ready, 8)
            cst = lambda n, lo=0, hi=P: CST[lo:hi, CONST_COLS[n][0]:CONST_COLS[n][1]]
            nc.vector.tensor_copy(identb[:], ident).then_inc(const_ready, 1)
            for n in masks:
                nc.vector.tensor_copy(masks[n][:], cst(n)).then_inc(const_ready, 1)
            nc.vector.tensor_copy(K1[MROW:P, :, :].rearrange("p h t -> p (h t)"), cst("pick1", MROW, P))\
                .then_inc(const_ready, 1)
            nc.vector.tensor_copy(K3[MROW:P, 0, :, :].rearrange("p h t -> p (h t)"), cst("pick3", MROW, P))\
                .then_inc(const_ready, 1)

            def norm(i, y, dst, s, base, n):
                for q in range(2):
                    nc.vector.bn_stats(stats[:, i, q, :], y[:, q, :]).then_inc(s, 1)
                dve.wait_ge(s, base + n + 2)
                nc.vector.memset(fence[:], 0.0)
                for q in range(2):
                    nc.vector.bn_aggr(mv[:, i, q, :], stats[:, i, q, :]).then_inc(s, 1)
                dve.wait_ge(s, base + n + 4)
                nc.vector.tensor_scalar(vare[:, i, :], mv[:, i, :, 1], EPS, None, ALU.add).then_inc(s, 1)

            def norm_end(i, y, dst, s, base, n, seq):
                dve.wait_ge(rstd_ready[i], seq + 1)
                for q in range(2):
                    nc.vector.tensor_scalar(dst[:, q, :], y[:, q, :], mv[:, i, q, 0:1], rstd[:, i, q:q + 1],
                                            ALU.subtract, ALU.mult).then_inc(s, 1)
                dve.wait_ge(s, base + n + 7)

            def split_max(nmax, nmaxp, heads, maxes, n_max, split, base):
                dve.wait_ge(maxes, n_max)
                nc.vector.tensor_copy(nmaxp[:, :, 0:heads], nmax[:]).then_inc(split, 1)
                dve.wait_ge(split, base + 1)
                nc.vector.tensor_tensor(nmaxp[:, :, heads:2 * heads], nmax[:], nmaxp[:, :, 0:heads],
                                        ALU.subtract).then_inc(split, 1)

            def spread_max(mrow, dst, heads, fill, ready, n, copied, base):
                dve.wait_ge(ready, n)
                nc.vector.tensor_copy(mrow[MROW:P, :], misc[MROW:P, fill % 2, :].bitcast(BF16)[:, 0:S])\
                    .then_inc(copied, 1)
                dve.wait_ge(copied, base + 1)
                nc.vector.tensor_copy(dst, mrow[MROW:P, :].unsqueeze(1).broadcast_to([32, heads, S]))\
                    .then_inc(copied, 1)

            def run(t):
                if on("C", t):
                    c = t - LAG["C"]
                    nc.vector.scalar_tensor_tensor(out=Y3[:], in0=X2[:], scalar=2.0, in1=B3o[:],
                                                   op0=ALU.mult, op1=ALU.add).then_inc(evac3, 1)
                    dve.wait_ge(proj3, 4 * c + 1)
                    for rows, k, t0, t1 in NESTED:
                        nc.vector.tensor_scalar(XN[0:rows, k, t0:t1], misc[0:rows, C1_FILL % 2, k * S + t0:k * S + t1],
                                                B3[0:rows, 0, k:k + 1], B3[0:rows, 1, k:k + 1],
                                                ALU.mult, ALU.add).then_inc(evac3, 1)
                    for i in range(2):
                        dve.wait_ge(high3, 4 * c + 2 * i + 2)
                        for m in range(2):
                            nc.vector.scalar_tensor_tensor(
                                out=rest3[:, i, m * S:m * S + S], in0=misc[:, (C1_FILL + 1 + i) % 2, m * S:m * S + S],
                                scalar=B3[:, 2 + i, m:m + 1], in1=parts3[:, i, 0, m, :],
                                op0=ALU.add, op1=ALU.subtract).then_inc(evac3, 1)
                    dve.wait_ge(proj3, 4 * c + 4)
                    nc.vector.tensor_tensor(V3[:], misc[:, (C1_FILL + 3) % 2, :].rearrange("p (m f) -> p m f", m=2),
                                            B3v[:].unsqueeze(1).broadcast_to([P, 2, D]), ALU.add).then_inc(evac3, 1)
                if on("A", t):
                    a = t - LAG["A"]
                    for j in range(N_SC1):
                        dve.wait_ge(scores1, N_SC1 * a + j + 1)
                        if j < 4:
                            dst, src = nmax1[:, 0, 4 * j:4 * j + 4], row_ps[:, j % 2, :].rearrange("p (h k) -> p h k", h=4)
                        else:
                            dst, src = (nmax1[:, 1, 2 * (j - 4):2 * (j - 4) + 2],
                                        row_ps[:, j % 2, :].rearrange("p (h k) -> p h k", h=2))
                        nc.vector.tensor_reduce(dst, src, AX.X, ALU.max, negate=True).then_inc(max1, 1)
                    split_max(nmax1, nmaxp1, H1, max1, N_SC1 * a + N_SC1, msplit1, 2 * a)
                if on("B", t):
                    b = t - LAG["B"]
                    dve.wait_ge(proj2, 5 * b + 3)
                    nc.vector.tensor_tensor(V2[:], misc[:, (B1_FILL + 2) % 2, :].rearrange("p (m f) -> p m f", m=2),
                                            B2v[:].unsqueeze(1).broadcast_to([P, 2, D]), ALU.add).then_inc(vev2, 1)
                    dve.wait_ge(proj2, 5 * b + 5)
                    for q, (lo, hi) in enumerate(((0, 128), (128, 384))):
                        nc.vector.tensor_reduce(nmax2[:, q:q + 1], misc[:, (B1_FILL + 4) % 2, lo:hi], AX.X, ALU.max,
                                                negate=True).then_inc(max2, 1)
                    dve.wait_ge(max2, 3 * b + 2)
                    nc.vector.tensor_scalar(bias2[:], nmax2[:], 1.0 / 16.0, None, ALU.mult).then_inc(max2, 1)
                if on("A", t):
                    a = t - LAG["A"]
                    spread_max(mrow1, Q1[MROW:P, :, :], H1, A3_FILL, mrows1, a + 1, mcopy1, 2 * a)
                    dve.wait_ge(pv1, 4 * a + 4)
                    nc.vector.reciprocal(rsum1[:].rearrange("p g t -> p (g t)"), sum_ps[:]).then_inc(norm1, 1)
                    dve.wait_ge(norm1, 2 * a + 1)
                    nc.vector.tensor_tensor(OT1[:].rearrange("p g t -> p (g t)"), o_ps[:],
                                            rsum1[:].rearrange("p g t -> p (g t)"), ALU.mult).then_inc(norm1, 1)
                if on("B", t):
                    b = t - LAG["B"]
                    dve.wait_ge(act2, N_ACT2 * b + 7)
                    nc.vector.reciprocal(rsum2[:], sum2[:]).then_inc(vev2b, 1)
                    dve.wait_ge(vev2b, b + 1)
                    dve.wait_ge(attn2, 2 * b + 2)
                    for q in range(2):
                        nc.vector.scalar_tensor_tensor(out=Y2[:, q, :], in0=misc[:, (B3_FILL + 1) % 2, q * D:q * D + D],
                                                       scalar=rsum2[:, q:q + 1], in1=X1[:, q, :],
                                                       op0=ALU.mult, op1=ALU.add).then_inc(ln2, 1)
                    dve.wait_ge(ln2, N_LN2 * b + 2)
                    norm(1, Y2, X2, ln2, N_LN2 * b, 2)
                    norm_end(1, Y2, X2, ln2, N_LN2 * b, 2, b)
                    norm(2, X2, Z2, ln2b, N_LN2B * b, 0)
                    norm_end(2, X2, Z2, ln2b, N_LN2B * b, 0, b)
                if on("C", t):
                    c = t - LAG["C"]
                    for j in range(N_SC3):
                        dve.wait_ge(scores3, N_SC3 * c + j + 1)
                        dst = nmax3[:, 0, 2 * j:2 * j + 2] if j < 4 else nmax3[:, 1, 0:2]
                        nc.vector.tensor_reduce(dst, row_ps[:, j % 2, :].rearrange("p (h k) -> p h k", h=2),
                                                AX.X, ALU.max, negate=True).then_inc(max3, 1)
                    split_max(nmax3, nmaxp3, H3, max3, N_SC3 * c + N_SC3, msplit3, 2 * c)
                if on("P", t):
                    for i in range(2):
                        dve.wait_ge(high1, 2 * t + i + 1)
                        nc.vector.tensor_tensor(rest1[:, i, :], misc[:, (P_FILL + i) % 2, :],
                                                parts1[:, i, 0, :, :].rearrange("p m t -> p (m t)"),
                                                ALU.subtract).then_inc(evac1, 1)
                    dve.wait_ge(proj1, 3 * t + 3)
                    v = misc[:, (P_FILL + 2) % 2, :].rearrange("p (kg w u d) -> p kg w u d", kg=4, w=2, u=4)
                    dst = V1[:].rearrange("p k (g w u) e -> p (k g) w u e", g=2, w=2)
                    for w in range(2):
                        nc.vector.tensor_copy(dst[:, :, w, :, D1 * w:D1 * w + D1], v[:, :, w, :, :]).then_inc(evac1, 1)
                if on("C", t):
                    c = t - LAG["C"]
                    spread_max(mrow3, Q3[MROW:P, 0, :, :], H3, C3_FILL, mrows3, c + 1, mcopy3, 2 * c)
                    dve.wait_ge(pv3, c + 1)
                    for rows, k, t0, t1 in NESTED:
                        nc.vector.reciprocal(rsum3[0:rows, k, t0:t1], sum_ps[0:rows, k * S + t0:k * S + t1])\
                            .then_inc(norm3, 1)
                    dve.wait_ge(norm3, 8 * c + 4)
                    for rows, k, t0, t1 in NESTED:
                        nc.vector.tensor_tensor(OT3[0:rows, k, t0:t1], o_ps[0:rows, k * S + t0:k * S + t1],
                                                rsum3[0:rows, k, t0:t1], ALU.mult).then_inc(norm3, 1)
                if on("A", t):
                    a = t - LAG["A"]
                    dve.wait_ge(attn1, a + 1)
                    dve.wait_ge(x_in, 16 * a + 16)
                    for q in range(2):
                        nc.vector.tensor_tensor(Y1[:, q, :], misc[:, A4_FILL % 2, q * D:q * D + D], XR[:, q, :],
                                                ALU.add).then_inc(ln1, 1)
                    dve.wait_ge(ln1, N_LN1 * a + 2)
                    norm(0, Y1, X1, ln1, N_LN1 * a, 2)
                    norm_end(0, Y1, X1, ln1, N_LN1 * a, 2, a)
                if on("C", t):
                    c = t - LAG["C"]
                    dve.wait_ge(attn3, c + 1)
                    for r0, r1, tile, f0, f1 in NESTED_OUT:
                        nc.vector.tensor_tensor(Y3[r0:r1, tile, f0:f1], misc[r0:r1, C4_FILL % 2, tile * D + f0:tile * D + f1],
                                                Y3[r0:r1, tile, f0:f1], ALU.add).then_inc(ln3, 1)
                    dve.wait_ge(ln3, N_LN3 * c + 4)
                    norm(3, Y3, OUT, ln3, N_LN3 * c, 4)
                    wait(dve, out_stored, 16 * c)
                    norm_end(3, Y3, OUT, ln3, N_LN3 * c, 4, c)

            steps(dve, run)

        @block.tensor
        def _(pe):
            mm = nc.tensor.matmul

            def tokens_by_feature(bank, w, xt, cols=None):
                for m in range(2):
                    for k in range(2):
                        n = S if cols is None or k == 0 else cols
                        last = mm(misc[:, bank, m * S:m * S + n], w[:, k, m * P:m * P + P], xt[:, k, 0:n],
                                  start=(k == 0), stop=(k == 1), skip_group_check=True)
                return last

            def features_by_token(bank, w, xt):
                for q in range(2):
                    for k in range(2):
                        last = mm(misc[:, bank, q * D:q * D + D], xt[:, k, q * P:q * P + P], w[:, k, 0:D],
                                  start=(k == 0), stop=(k == 1))
                return last

            def turn(bank, src):
                for k in range(2):
                    for q in range(2):
                        last = nc.tensor.transpose(misc[:, bank, k * S + q * P:k * S + q * P + P],
                                                   src[:, q, k * P:k * P + P], ident)
                return last

            def C1(t):
                c = t - LAG["C"]
                pe.wait_ge(ln2b, N_LN2B * c + 7)
                misc_free(pe, t, C1_FILL)
                turn(C1_FILL % 2, Z2).then_inc(proj3, 1)
                pe.wait_ge(evac3, N_EV3 * c + 5)
                for i, w in enumerate((W3q, W3k)):
                    misc_free(pe, t, C1_FILL + 1 + i)
                    tokens_by_feature((C1_FILL + 1 + i) % 2, w, XN, P).then_inc(proj3, 1)
                misc_free(pe, t, C1_FILL + 3)
                bank = (C1_FILL + 3) % 2
                mm(misc[:, bank, 0:D], XN[:, 0, 0:P], W3v[:, 0, :], start=True, stop=False)
                mm(misc[:, bank, 0:D], XN[:, 1, 0:P], W3v[:, 1, :], start=False, stop=True)
                mm(misc[:, bank, D:2 * D], XN[:, 0, P:S], W3v[:, 0, :], start=True, stop=True).then_inc(proj3, 1)

            def A2(t):
                a = t - LAG["A"]
                pe.wait_ge(stacks1_in, 192 * a + 192)
                for j in range(N_SC1):
                    bank = row_ps[:, j % 2, :]
                    if j >= 2:
                        pe.wait_ge(max1, N_SC1 * a + j - 1)
                    else:
                        if not fixed(t) or t > LAG["C"]:
                            pe.wait_ge(max3, N_SC3 * (t - LAG["C"]))
                        if fixed(a):
                            wait(pe, max1, N_SC1 * a)
                    if j < 4:
                        mm(bank, identb[:], masks["mask_q0"][:], start=True, stop=False)
                        for u in range(4):
                            h = 4 * j + u
                            last = mm(bank[:, u * P:u * P + P], Q1[0:MROW, h, 0:P], K1[0:MROW, h, 0:P],
                                      start=False, stop=(u == 3))
                    else:
                        mm(bank, identb[:], masks["mask_q1"][:], start=True, stop=False)
                        for u in range(2):
                            h = 2 * (j - 4) + u
                            last = mm(bank[:, u * S:u * S + S], Q1[0:MROW, h, P:S], K1[0:MROW, h, :],
                                      start=False, stop=(u == 1))
                    last.then_inc(scores1, 1)

            def B1(t):
                b = t - LAG["B"]
                pe.wait_ge(ln1, N_LN1 * b + N_LN1)
                misc_free(pe, t, B1_FILL)
                turn(B1_FILL % 2, X1).then_inc(proj2, 1)
                pe.wait_ge(ctxT_in, 16 * b + 16)
                misc_free(pe, t, B1_FILL + 1)
                tokens_by_feature((B1_FILL + 1) % 2, W2k, CT).then_inc(proj2, 1)
                misc_free(pe, t, B1_FILL + 2)
                features_by_token((B1_FILL + 2) % 2, W2v, CT).then_inc(proj2, 1)
                pe.wait_ge(act2, N_ACT2 * b + 1)
                misc_free(pe, t, B1_FILL + 3)
                tokens_by_feature((B1_FILL + 3) % 2, W2q, X1T).then_inc(proj2, 1)
                pe.wait_ge(act2, N_ACT2 * b + 5)
                misc_free(pe, t, B1_FILL + 4)
                bank = misc[:, (B1_FILL + 4) % 2, :]
                mm(bank[:, 0:P], identb[:], masks["mask_q0"][:, 0:P], start=True, stop=False)
                for k in range(2):
                    mm(bank[:, 0:P], Q2[:, k, 0:P], K2[:, k, 0:P], start=False, stop=(k == 1))
                mm(bank[:, S:S + P], identb[:], masks["mask_q0"][:, 0:P], start=True, stop=False,
                   skip_group_check=True)
                for k in range(2):
                    last = mm(bank[:, P:P + S], Q2[:, k, P:S], K2[:, k, :], start=False, stop=(k == 1),
                              skip_group_check=True)
                last.then_inc(proj2, 1)

            def A3(t):
                a = t - LAG["A"]
                misc_free(pe, t, A3_FILL)
                pe.wait_ge(msplit1, 2 * a + 2)
                rows = misc[MROW:P, A3_FILL % 2, :].bitcast(BF16)
                for q in range(2):
                    last = nc.tensor.transpose(rows[:, q * P:q * P + P], nmaxp1[:, q, :], identb[:])
                last.then_inc(mrows1, 1)

                def scores(g, f):
                    j = 3 * g + f
                    bank = col_ps[:, j % 2, :]
                    if j == 0:
                        pe.wait_ge(mcopy1, 2 * a + 2)
                    if j >= 2:
                        pe.wait_ge(exp1, N_T1 * a + j - 1)
                    else:
                        if not fixed(t) or t > LAG["C"]:
                            pe.wait_ge(exp3, N_T3 * (t - LAG["C"]))
                        if fixed(a):
                            wait(pe, exp1, N_T1 * a)
                    mm(bank, identb[:], masks["mask_k1" if f == 2 else "mask_k0"][:], start=True, stop=False)
                    if f < 2:
                        for u in range(2):
                            h = 4 * g + 2 * f + u
                            last = mm(bank[:, u * S:u * S + S], K1[:, h, 0:P], Q1[:, h, :], start=False, stop=(u == 1))
                    else:
                        for u in range(4):
                            h = 4 * g + u
                            last = mm(bank[:, u * P:u * P + P], K1[:, h, P:S], Q1[:, h, P:S], start=False, stop=(u == 3))
                    last.then_inc(scoresT1, 1)

                def products(g, f):
                    p = PT1[:, g % 2, :, :]
                    even = g % 2 == 0
                    o0 = (g // 2) * S
                    ones = ones_lo if even else ones_hi
                    if g == 0 and f == 0:
                        if not fixed(t) or t > LAG["C"]:
                            pe.wait_ge(norm3, 8 * (t - LAG["C"]))
                        if fixed(a):
                            wait(pe, norm1, 2 * a)
                    if f < 2:
                        pe.wait_ge(exp1, N_T1 * a + 3 * g + 2)
                        for u in range(4):
                            q = slice(32 * u, 32 * u + 32)
                            w = V1[:, 0, 4 * g + u, :] if f == 0 else ones
                            last = mm((o_ps if f == 0 else sum_ps)[q, o0:o0 + S], w,
                                      p[:, u // 2, (u % 2) * S:(u % 2) * S + S], start=even, stop=False)
                    else:
                        pe.wait_ge(exp1, N_T1 * a + 3 * g + 3)
                        for w1, dst in ((None, o_ps), (ones, sum_ps)):
                            for u in range(4):
                                q = slice(32 * u, 32 * u + 32)
                                w = V1[:, 1, 4 * g + u, :] if w1 is None else w1
                                last = mm(dst[q, o0 + P:o0 + S], w, p[:, 2, u * P:u * P + P],
                                          start=False, stop=not even)
                        last.then_inc(pv1, 1)

                for g in range(5):
                    for f in range(3):
                        if g < 4:
                            scores(g, f)
                        if g > 0:
                            products(g - 1, f)

            def B3p(t):
                b = t - LAG["B"]
                pe.wait_ge(act2, N_ACT2 * b + 7)
                misc_free(pe, t, B3_FILL)
                for i in range(3):
                    last = nc.tensor.transpose(misc[:, B3_FILL % 2, i * P:i * P + P], P2[:, i, :], ident)
                last.then_inc(attn2, 1)
                misc_free(pe, t, B3_FILL + 1)
                pe.wait_ge(pT2, b + 1)
                bank = (B3_FILL + 1) % 2
                mm(misc[:, bank, 0:D], PT2[:, 0, :], V2[:, 0, :], start=True, stop=True)
                mm(misc[:, bank, D:2 * D], PT2[:, 1, :], V2[:, 0, :], start=True, stop=False)
                mm(misc[:, bank, D:2 * D], PT2[:, 2, :], V2[:, 1, :], start=False, stop=True).then_inc(attn2, 1)

            def C2(t):
                c = t - LAG["C"]
                pe.wait_ge(stacks3_in, 192 * c + 192)
                for j in range(N_SC3):
                    if j >= 2:
                        pe.wait_ge(max3, N_SC3 * c + j - 1)
                    else:
                        a = min(t - LAG["A"], NB - 1) if fixed(t) else t - LAG["A"]
                        pe.wait_ge(max1, N_SC1 * (a + 1))
                        if fixed(c):
                            wait(pe, max3, N_SC3 * c)
                    q, h0 = (0, 2 * j) if j < 4 else (1, 0)
                    for u in range(2):
                        for s in range(2):
                            last = mm(row_ps[:, j % 2, u * S:u * S + S], Q3[0:MROW, s, h0 + u, q * P:q * P + P],
                                      K3[0:MROW, s, h0 + u, :], start=(s == 0), stop=(s == 1))
                    last.then_inc(scores3, 1)

            def Pp(t):
                pe.wait_ge(xT_in, 16 * t + 16)
                for i in range(2):
                    misc_free(pe, t, P_FILL + i)
                    tokens_by_feature((P_FILL + i) % 2, W1[:, :, i * D:i * D + D], XT).then_inc(proj1, 1)
                misc_free(pe, t, P_FILL + 2)
                features_by_token((P_FILL + 2) % 2, W1[:, :, 2 * D:3 * D], XT).then_inc(proj1, 1)

            def C3(t):
                c = t - LAG["C"]
                misc_free(pe, t, C3_FILL)
                pe.wait_ge(msplit3, 2 * c + 2)
                rows = misc[MROW:P, C3_FILL % 2, :].bitcast(BF16)
                for q in range(2):
                    last = nc.tensor.transpose(rows[:, q * P:q * P + P], nmaxp3[:, q, :], identb[:])
                last.then_inc(mrows3, 1)
                pe.wait_ge(mcopy3, 2 * c + 2)
                for j in range(N_T3):
                    if j >= 2:
                        pe.wait_ge(exp3, N_T3 * c + j - 1)
                    else:
                        a = min(t - LAG["A"], NB - 1) if fixed(t) else t - LAG["A"]
                        pe.wait_ge(exp1, N_T1 * (a + 1))
                        if fixed(c):
                            wait(pe, exp3, N_T3 * c)
                    keys = slice((j // 2) * P, (j // 2) * P + P)
                    for h, col in T3_BANKS[j % 2]:
                        n = Q3_USED[h]
                        for s, rows_used in ((0, P), (1, MROW)):
                            last = mm(col_ps[:, j % 2, col:col + n], K3[0:rows_used, s, h, keys],
                                      Q3[0:rows_used, s, h, 0:n], start=(s == 0), stop=(s == 1))
                    last.then_inc(scoresT3, 1)
                a = min(t - LAG["A"], NB - 1) if fixed(t) else t - LAG["A"]
                pe.wait_ge(norm1, 2 * a + 2)
                if fixed(c):
                    wait(pe, norm3, 8 * c)
                place = {h: (f, col) for f in range(2) for h, col in T3_BANKS[f]}
                for half in range(2):
                    for k in range(2):
                        pe.wait_ge(exp3, N_T3 * c + 2 * k + 2)
                        for values in (True, False):
                            for u in range(4):
                                h = 4 * half + u
                                f, col = place[h]
                                n = Q3_USED[h]
                                w = V3[:, k, D3 * h:D3 * h + D3] if values else ones32[:]
                                last = mm((o_ps if values else sum_ps)[32 * u:32 * u + 32, half * S:half * S + n], w,
                                          PT3[:, k, f, col:col + n], start=(k == 0), stop=(k == 1))
                last.then_inc(pv3, 1)

            def A4(t):
                a = t - LAG["A"]
                pe.wait_ge(norm1, 2 * a + 2)
                misc_free(pe, t, A4_FILL)
                features_by_token(A4_FILL % 2, W1o, OT1).then_inc(attn1, 1)

            def C4(t):
                c = t - LAG["C"]
                pe.wait_ge(norm3, 8 * c + 8)
                misc_free(pe, t, C4_FILL)
                bank = C4_FILL % 2
                mm(misc[:, bank, 0:D], OT3[:, 0, 0:P], W3o[:, 0, :], start=True, stop=False)
                mm(misc[:, bank, 0:D], OT3[:, 1, 0:P], W3o[:, 1, :], start=False, stop=True)
                mm(misc[:, bank, D:D + P], OT3[:, 0, P:S], W3o[:, 0, 0:P], start=True, stop=True).then_inc(attn3, 1)

            def run(t):
                for stage, phase in (("C", C1), ("A", A2), ("B", B1), ("A", A3), ("B", B3p),
                                     ("C", C2), ("P", Pp), ("C", C3), ("A", A4), ("C", C4)):
                    if on(stage, t):
                        phase(t)

            pe.wait_ge(weights_in, 16 * 18)
            pe.wait_ge(const_ready, 7)
            steps(pe, run)


def layer_constants():
    import numpy as np
    c = np.zeros((P, CONST_W), np.float32)

    def put(name, a, rows=slice(None)):
        c[rows, CONST_COLS[name][0]:CONST_COLS[name][1]] = a

    i, j = np.arange(P)[:, None], np.arange(P)[None, :]
    causal = np.where(j <= i, 0.0, NEG)
    band = np.where((j > i) | (j < PREFIX), 0.0, NEG)
    put("ident", np.eye(P))
    put("mask_q0", np.tile(causal, (1, 4)))
    put("mask_q1", np.tile(np.concatenate([band, causal], 1), (1, 2)))
    put("mask_k0", np.tile(np.concatenate([causal.T, band.T], 1), (1, 2)))
    put("mask_k1", np.tile(causal.T, (1, 4)))
    ones = np.zeros((P, 64))
    ones[:, 0:D1] = 1.0
    ones[:, 32 + D1:64] = 1.0
    put("ones", ones)
    for name, heads in (("pick1", H1), ("pick3", H3)):
        pick = np.zeros((32, heads, S))
        for h in range(heads):
            pick[[h, heads + h], h, :] = 1.0
        put(name, pick.reshape(32, heads * S), slice(MROW, P))
    return c


def kernel(**inputs):
    import numpy as np
    import concourse.bacc as bacc
    from concourse.bass_utils import run_bass_kernel_spmd

    g = {k: np.asarray(v) for k, v in inputs.items()}
    nc = bacc.Bacc("TRN2", target_bir_lowering=False, num_devices=1)

    def by_feature(a):
        return a.reshape(NB * S, 2, P).transpose(2, 1, 0)

    def by_token(a):
        return a.reshape(NB * 2, P, D).transpose(1, 0, 2)

    def halves(*vs):
        return np.stack([v.reshape(2, P) for v in vs]).transpose(2, 0, 1)

    w_out = g["L0_attn_w_out"].T.reshape(2, 2, 4, D1, D).transpose(0, 2, 1, 3, 4).reshape(D, D)
    arrays = {
        "xT": by_feature(g["x"]), "x": by_token(g["x"]), "ctxT": by_feature(g["ctx_1024"]),
        "consts": layer_constants(),
        "w1_qkvT": g["L0_attn_w_qkv"].T, "w1_oT": w_out,
        "w2_qT": g["L0_xattn_wq_w"].T, "w2_kT": g["L0_xattn_wk_w"].T, "w2_vT": g["L0_xattn_wv_w"].T,
        "b2": halves(g["L0_xattn_wq_b"], g["L0_xattn_wk_b"]), "bv2": g["L0_xattn_wv_b"],
        "w3_qT": g["L0_ffn_q_w"].T, "w3_kT": g["L0_ffn_k_w"].T, "w3_vT": g["L0_ffn_v_w"].T,
        "w3_oT": g["L0_ffn_o_w"].T,
        "b3": halves(g["L0_ffn_norm_w"], g["L0_ffn_norm_b"], g["L0_ffn_q_b"], g["L0_ffn_k_b"]),
        "bv3": g["L0_ffn_v_b"], "bo3": g["L0_ffn_o_b"],
    }
    arrays = {k: np.ascontiguousarray(v) for k, v in arrays.items()}
    args = [nc.dram_tensor(f"in_{k}", v.shape, mybir.dt.from_np(v.dtype), kind="ExternalInput").ap()
            for k, v in arrays.items()]
    out = nc.dram_tensor("out", (P, NB * 2, D), F32, kind="ExternalOutput").ap()
    build(nc, *args, out)
    r = run_bass_kernel_spmd(nc, [{f"in_{k}": v for k, v in arrays.items()}], core_ids=[0])
    got = np.asarray(r.results[0]["out"])
    return got.transpose(1, 0, 2).reshape(NB, S, D)
```

```python
from contextlib import ExitStack

import concourse.bass as bass
from concourse import mybir

F32 = mybir.dt.float32
BF16 = mybir.dt.bfloat16
ALU = mybir.AluOpType
ACT = mybir.ActivationFunctionType
AX = mybir.AxisListType

NB, S, D = 16, 256, 256
P = 128
H1, D1 = 16, D // 16
H3, D3 = 8, D // 8
PREFIX = 16
EPS = 1e-5
NEG = -1.0e30

Q1_PARTS, K1_PARTS = (0, 0, 1, 1, 0, 2), (0, 1, 0, 1, 2, 0)
Q3_PARTS, K3_PARTS = ((0, 0, 1), (1, 0, 2)), ((0, 1, 0), (1, 2, 0))
MROW = 96

NESTED = ((128, 0, 0, 128), (64, 0, 128, 192), (32, 0, 192, 256), (128, 1, 0, 64))
NESTED_OUT = ((0, 128, 0, 0, 128), (0, 64, 0, 128, 256), (0, 64, 1, 0, 64), (64, 128, 1, 0, 32))
Q3_USED = (256, 192, 128, 128, 64, 64, 64, 64)
T3_BANKS = (((0, 0), (1, 256), (4, 448)), ((2, 0), (3, 128), (5, 256), (6, 320), (7, 384)))
T3_COLS = (512, 448)

LAG = {"P": 0, "A": 1, "B1": 1, "B3": 2, "C1": 2, "C": 3}

CONST_COLS = {}
_at = 0
for _name, _n in (("ident", 128), ("mask_q0", 512), ("mask_q1", 512), ("mask_k0", 512),
                  ("mask_k1", 512), ("ones", 64), ("pick1", H1 * S), ("pick3", H3 * S)):
    CONST_COLS[_name] = (_at, _at + _n)
    _at += _n
CONST_W = _at


def build(nc, xT, x, ctxT, consts, w1_qkvT, w1_oT, w2_qT, w2_kT, w2_vT, b2, bv2, w3_qT, w3_kT, w3_vT,
          w3_oT, b3, bv3, bo3, out):
    with ExitStack() as ctx:
        def sb(name, shape, dt=F32):
            return ctx.enter_context(nc.sbuf_tensor(name, shape, dt))

        def psum(name, shape):
            return ctx.enter_context(nc.psum_tensor(name, shape, F32))

        def sem(name):
            return ctx.enter_context(nc.semaphore(name))

        parts1_dram = nc.dram_tensor("parts1_dram", [6, D, S], BF16, kind="Internal").ap()
        parts3_dram = nc.dram_tensor("parts3_dram", [6, D, S], BF16, kind="Internal").ap()

        W1 = sb("W1", [P, 2, 3 * D])
        W1o = sb("W1o", [P, 2, D])
        W2q, W2k, W2v = sb("W2q", [P, 2, D]), sb("W2k", [P, 2, D]), sb("W2v", [P, 2, D])
        W3q, W3k, W3v, W3o = (sb(n, [P, 2, D]) for n in ("W3q", "W3k", "W3v", "W3o"))
        B2 = sb("B2", [P, 2, 2])
        B2v = sb("B2v", [P, D])
        B3 = sb("B3", [P, 4, 2])
        B3v = sb("B3v", [P, D])
        B3o = sb("B3o", [P, 2, D])
        CST = sb("CST", [P, CONST_W])
        ident = CST[:, CONST_COLS["ident"][0]:CONST_COLS["ident"][1]]
        identb = sb("identb", [P, P], BF16)
        masks = {n: sb(n, [P, 512], BF16) for n in ("mask_q0", "mask_q1", "mask_k0", "mask_k1")}
        ones_lo = CST[:, CONST_COLS["ones"][0]:CONST_COLS["ones"][0] + 32]
        ones_hi = CST[:, CONST_COLS["ones"][0] + 32:CONST_COLS["ones"][1]]
        ones32 = sb("ones32", [P, 32])
        minus_half = sb("minus_half", [P, 2])

        XT = sb("XT", [P, 2, S])
        XR = sb("XR", [P, 2, D])
        parts1 = sb("parts1", [P, 2, 3, 2, S], BF16)
        rest1 = sb("rest1", [P, 2, 2 * S])
        V1 = sb("V1", [P, 2, H1, 32])
        Q1, K1 = sb("Q1", [P, H1, S], BF16), sb("K1", [P, H1, S], BF16)
        nmax1 = sb("nmax1", [P, 2, H1])
        nmaxp1 = sb("nmaxp1", [P, 2, 32], BF16)
        mrow1 = sb("mrow1", [P, S], BF16)
        PT1 = sb("PT1", [P, 2, 3, 512])
        rsum1 = sb("rsum1", [P, 2, S])
        OT1 = sb("OT1", [P, 2, S])
        Y1, X1 = sb("Y1", [P, 2, D]), sb("X1", [P, 2, D])
        CT = sb("CT", [P, 2, S])
        X1T, Q2, K2 = sb("X1T", [P, 2, S]), sb("Q2", [P, 2, S]), sb("K2", [P, 2, S])
        V2 = sb("V2", [P, 2, D])
        nmax2, bias2 = sb("nmax2", [P, 2]), sb("bias2", [P, 2])
        sum2, rsum2 = sb("sum2", [P, 2]), sb("rsum2", [P, 2])
        P2, PT2 = sb("P2", [P, 3, P]), sb("PT2", [P, 3, P])
        Y2, X2, Z2 = sb("Y2", [P, 2, D]), sb("X2", [P, 2, D]), sb("Z2", [P, 2, D])
        XN = sb("XN", [P, 2, S])
        parts3 = sb("parts3", [P, 2, 3, 2, S], BF16)
        rest3 = sb("rest3", [P, 2, 2 * S])
        V3 = sb("V3", [P, 2, D])
        Q3, K3 = sb("Q3", [P, 2, H3, S], BF16), sb("K3", [P, 2, H3, S], BF16)
        nmax3 = sb("nmax3", [P, 2, H3])
        nmaxp3 = sb("nmaxp3", [P, 2, 32], BF16)
        mrow3 = sb("mrow3", [P, S], BF16)
        PT3 = sb("PT3", [P, 2, 2, 512])
        rsum3 = sb("rsum3", [P, 2, S])
        OT3 = sb("OT3", [P, 2, S])
        Y3, OUT = sb("Y3", [P, 2, D]), sb("OUT", [P, 2, D])
        stats = sb("stats", [P, 4, 2, 6])
        mv = sb("mv", [P, 4, 2, 2])
        vare = sb("vare", [P, 4, 2])
        rstd = sb("rstd", [P, 4, 2])
        fence = sb("fence", [P, 1])

        row_ps = psum("row_ps", [P, 2, 512])
        col_ps = psum("col_ps", [P, 2, 512])
        acc = psum("acc", [P, 2, 2, S])
        misc = psum("misc", [P, 2, 512])

        weights_in = sem("weights_in")
        xT_in, x_in, ctxT_in = sem("xT_in"), sem("x_in"), sem("ctxT_in")
        q_out1, k_out1, q_out3, k_out3 = (sem(n) for n in ("q_out1", "k_out1", "q_out3", "k_out3"))
        stacks1_in, stacks3_in = sem("stacks1_in"), sem("stacks3_in")
        out_stored = sem("out_stored")
        const_ready, pool_ready = sem("const_ready"), sem("pool_ready")
        proj1, scores1, mrows1, scoresT1, pv1, attn1 = (
            sem(n) for n in ("proj1", "scores1", "mrows1", "scoresT1", "pv1", "attn1"))
        proj2, attn2 = sem("proj2"), sem("attn2")
        proj3, scores3, mrows3, scoresT3, pv3, attn3 = (
            sem(n) for n in ("proj3", "scores3", "mrows3", "scoresT3", "pv3", "attn3"))
        high1, mid1, exp1 = sem("high1"), sem("mid1"), sem("exp1")
        act2, pT2 = sem("act2"), sem("pT2")
        high3, mid3, exp3 = sem("high3"), sem("mid3"), sem("exp3")
        low1, low3 = sem("low1"), sem("low3")
        rstd_ready = [sem(f"rstd_ready{i}") for i in range(4)]
        evac1, max1, msplit1, mcopy1, norm1, ln1 = (
            sem(n) for n in ("evac1", "max1", "msplit1", "mcopy1", "norm1", "ln1"))
        vev2, rec2, max2, ln2, ln2b = sem("vev2"), sem("rec2"), sem("max2"), sem("ln2"), sem("ln2b")
        evac3, max3, msplit3, mcopy3, norm3, ln3 = (
            sem(n) for n in ("evac3", "max3", "msplit3", "mcopy3", "norm3", "ln3"))

        N_EV1, N_EV3, N_ACT2, N_LN1, N_LN2, N_LN2B, N_LN3 = 4, 10, 7, 9, 9, 7, 11
        N_SC1, N_SC3, N_T1, N_T3 = 12, 5, 12, 4

        MISC = [("A", mcopy1, 2, 1),
                ("P", evac1, N_EV1, 1), ("P", evac1, N_EV1, 2),
                ("C", mcopy3, 2, 1),
                ("B3", pT2, 1, 1), ("B3", ln2, N_LN2, 2),
                ("P", evac1, N_EV1, 4),
                ("C", ln3, N_LN3, 4),
                ("C1", evac3, N_EV3, 4),
                ("A", ln1, N_LN1, 2),
                ("C1", evac3, N_EV3, 6), ("C1", evac3, N_EV3, 8), ("C1", evac3, N_EV3, 9),
                ("B1", act2, N_ACT2, 2), ("B1", vev2, 1, 1), ("B1", act2, N_ACT2, 3), ("B1", act2, N_ACT2, 5),
                ("B1", act2, N_ACT2, 7)]
        M1_FILL, PQ_FILL, M3_FILL, PT2_FILL, Y2_FILL, PV_FILL = 0, 1, 3, 4, 5, 6
        C4_FILL, Z_FILL, A4_FILL, C1_FILL = 7, 8, 9, 10
        K2_FILL, V2_FILL, XT_FILL, Q2_FILL, S2_FILL = 13, 14, 15, 16, 17

        def fixed(t):
            return type(t) is int

        def on(stage, t):
            return not fixed(t) or 0 <= t - LAG[stage] < NB

        def wait(eng, s, n):
            if not fixed(n) or n > 0:
                eng.wait_ge(s, n)

        def misc_free(pe, t, n):
            stage, s, per, after = MISC[n - 2]
            seq = t - LAG[stage] - (1 if n < 2 else 0)
            if not fixed(t):
                pe.wait_ge(s, seq * per + after)
                return
            for m, (stage, s, per, after) in enumerate(MISC):
                if m % 2 == n % 2:
                    seq = min(t - LAG[stage] - (0 if m < n else 1), NB - 1)
                    if seq >= 0:
                        pe.wait_ge(s, seq * per + after)
            return

        def steps(eng, run):
            for t in range(4):
                run(t)
            with eng.Fori(4, NB) as t:
                run(t)
            for t in range(NB, NB + LAG["C"]):
                run(t)

        block = ctx.enter_context(nc.Block())

        @block.sync
        def _(sp):
            n = 0

            def load(dst, src):
                sp.dma_start(dst, src).then_inc(weights_in, 16)

            load(W1[:], w1_qkvT.rearrange("(k p) o -> p k o", p=P))
            load(CST[:], consts)
            for dst, src in ((W1o, w1_oT), (W2q, w2_qT), (W2k, w2_kT), (W2v, w2_vT),
                             (W3q, w3_qT), (W3k, w3_kT), (W3v, w3_vT), (W3o, w3_oT)):
                load(dst[:], src.rearrange("(k p) o -> p k o", p=P))
            load(B2[:], b2)
            load(B3[:], b3)
            load(B2v[:], bv2.partition_broadcast(P))
            load(B3v[:], bv3.partition_broadcast(P))
            sp.wait_ge(pool_ready, 1)
            for r0, r1, tile, f0, f1 in NESTED_OUT:
                load(B3o[r0:r1, tile, f0:f1], bo3[f0:f1].partition_broadcast(r1 - r0))

            def run(t):
                p, a, b, c1, c = (t - LAG[x] for x in ("P", "A", "B1", "C1", "C"))

                def count(n):
                    return n if fixed(n) else sp.snap(n)

                def bounce_out(scratch, parts, i, wrote):
                    sp.dma_start(scratch[3 * i:3 * i + 3].rearrange("s (m p) t -> p s m t", p=P),
                                 parts[:, i, :, :, :]).then_inc(wrote, 16)

                def stack(dst, scratch, which, width, landed):
                    for r, part in enumerate(which):
                        sp.dma_start(dst[width * r:width * r + width, :, :], scratch[part].rearrange(
                            "(h d) t -> d h t", d=width)).then_inc(landed, 16)

                if on("P", t):
                    wait(sp, proj1, count(3 * p))
                    sp.dma_start(XT[:], xT[:, :, bass.ds(count(p * S), S)]).then_inc(xT_in, 16)
                if on("B1", t):
                    wait(sp, proj2, count(5 * b))
                    sp.dma_start(CT[:], ctxT[:, :, bass.ds(count(b * S), S)]).then_inc(ctxT_in, 16)
                if on("A", t):
                    wait(sp, ln1, count((a - 1) * N_LN1 + 2))
                    sp.dma_start(XR[:], x[:, bass.ds(count(a * 2), 2), :]).then_inc(x_in, 16)
                if on("P", t):
                    wait(sp, stacks1_in, count(192 * p))
                    sp.wait_ge(low1, count(2 * p + 1))
                    bounce_out(parts1_dram, parts1, 0, q_out1)
                    sp.wait_ge(low1, count(2 * p + 2))
                    bounce_out(parts1_dram, parts1, 1, k_out1)
                    if on("A", t):
                        sp.wait_ge(scoresT1, count(N_T1 * a + N_T1))
                    elif fixed(t) and t > LAG["A"]:
                        sp.wait_ge(scoresT1, N_T1 * NB)
                    sp.wait_ge(q_out1, count(16 * p + 16))
                    stack(Q1, parts1_dram, Q1_PARTS, D1, stacks1_in)
                    sp.wait_ge(k_out1, count(16 * p + 16))
                    stack(K1, parts1_dram, [3 + x for x in K1_PARTS], D1, stacks1_in)
                if on("C1", t):
                    wait(sp, pv3, count(c1))
                    sp.wait_ge(low3, count(2 * c1 + 1))
                    bounce_out(parts3_dram, parts3, 0, q_out3)
                    sp.wait_ge(low3, count(2 * c1 + 2))
                    bounce_out(parts3_dram, parts3, 1, k_out3)
                    sp.wait_ge(q_out3, count(16 * c1 + 16))
                    for j in range(2):
                        stack(Q3[:, j, :, :], parts3_dram, Q3_PARTS[j], D3, stacks3_in)
                    sp.wait_ge(k_out3, count(16 * c1 + 16))
                    for j in range(2):
                        stack(K3[:, j, :, :], parts3_dram, [3 + x for x in K3_PARTS[j]], D3, stacks3_in)
                if on("C", t):
                    sp.wait_ge(ln3, count(N_LN3 * c + N_LN3))
                    sp.dma_start(out[:, bass.ds(count(c * 2), 2), :], OUT[:]).then_inc(out_stored, 16)

            steps(sp, run)
            sp.wait_ge(out_stored, 16 * NB)

        @block.gpsimd
        def _(pool):
            nc.gpsimd.memset(B3o[:], 0.0).then_inc(pool_ready, 1)
            for zeroed in (V1, XN, OT3, nmax3, nmaxp3):
                nc.gpsimd.memset(zeroed[:], 0.0).then_inc(pool_ready, 1)
            nc.gpsimd.memset(ones32[:], 1.0).then_inc(pool_ready, 1)
            nc.gpsimd.memset(minus_half[:], -0.5).then_inc(pool_ready, 1)
            pool.wait_ge(pool_ready, 8)

            def low_part(rest, parts, mid, low, i, n):
                pool.wait_ge(mid, n)
                nc.gpsimd.tensor_tensor(parts[:, i, 2, :, :].rearrange("p m t -> p (m t)"), rest[:, i, :],
                                        parts[:, i, 1, :, :].rearrange("p m t -> p (m t)"),
                                        ALU.subtract).then_inc(low, 1)

            def root(i, ready, n):
                pool.wait_ge(ready, n)
                nc.gpsimd.tensor_tensor(rstd[:, i, :], vare[:, i, :], minus_half[:], ALU.pow)\
                    .then_inc(rstd_ready[i], 1)

            def run(t):
                p, a, b, c1, c = (t - LAG[x] for x in ("P", "A", "B3", "C1", "C"))
                if on("P", t):
                    for i in range(2):
                        low_part(rest1, parts1, mid1, low1, i, 2 * p + i + 1)
                if on("B3", t):
                    root(1, ln2, N_LN2 * b + 7)
                    root(2, ln2b, N_LN2B * b + 5)
                if on("A", t):
                    root(0, ln1, N_LN1 * a + 7)
                if on("C1", t):
                    for i in range(2):
                        low_part(rest3, parts3, mid3, low3, i, 2 * c1 + i + 1)
                if on("C", t):
                    root(3, ln3, N_LN3 * c + 9)

            steps(pool, run)

        @block.scalar
        def _(act):
            act.wait_ge(weights_in, 16 * 18)

            def mid_part(rest, parts, evac, n, mid, i):
                act.wait_ge(evac, n)
                nc.scalar.activation(parts[:, i, 1, :, :].rearrange("p m t -> p (m t)"), rest[:, i, :],
                                     ACT.Copy).then_inc(mid, 1)

            def run(t):
                if on("P", t):
                    for i in range(2):
                        act.wait_ge(proj1, 3 * t + 1 + i)
                        nc.scalar.activation(parts1[:, i, 0, :, :].rearrange("p m t -> p (m t)"),
                                             misc[:, (PQ_FILL + i) % 2, :], ACT.Copy).then_inc(high1, 1)
                    for i in range(2):
                        mid_part(rest1, parts1, evac1, N_EV1 * t + 1 + i, mid1, i)
                if on("B3", t):
                    b = t - LAG["B3"]
                    act.wait_ge(attn2, 2 * b + 1)
                    nc.scalar.activation(PT2[:].rearrange("p c k -> p (c k)"), misc[:, PT2_FILL % 2, 0:384],
                                         ACT.Copy).then_inc(pT2, 1)
                if on("C", t):
                    c = t - LAG["C"]
                    for j in range(N_T3):
                        act.wait_ge(scoresT3, N_T3 * c + j + 1)
                        n = T3_COLS[j % 2]
                        nc.scalar.activation(PT3[:, j // 2, j % 2, 0:n], col_ps[:, j % 2, 0:n], ACT.Exp,
                                             scale=1.0 / 16.0).then_inc(exp3, 1)
                if on("A", t):
                    a = t - LAG["A"]
                    for j in range(N_T1):
                        act.wait_ge(scoresT1, N_T1 * a + j + 1)
                        if j % 3 == 0:
                            wait(act, pv1, 4 * a - 1 + j // 3)
                        nc.scalar.activation(PT1[:, (j // 3) % 2, j % 3, :], col_ps[:, j % 2, :], ACT.Exp,
                                             scale=0.25).then_inc(exp1, 1)
                if on("C1", t):
                    c = t - LAG["C1"]
                    for i in range(2):
                        act.wait_ge(proj3, 4 * c + 2 + i)
                        for m in range(2):
                            nc.scalar.activation(parts3[:, i, 0, m, :], misc[:, (C1_FILL + i) % 2, m * S:m * S + S],
                                                 ACT.Identity, bias=B3[:, 2 + i, m:m + 1]).then_inc(high3, 1)
                        mid_part(rest3, parts3, evac3, N_EV3 * c + 6 + 2 * i, mid3, i)
                if on("B1", t):
                    b = t - LAG["B1"]

                    def biased(dst, i, fill, n):
                        act.wait_ge(proj2, 5 * b + n)
                        for m in range(2):
                            nc.scalar.activation(dst[:, m, :], misc[:, fill % 2, m * S:m * S + S],
                                                 ACT.Identity, bias=B2[:, i, m:m + 1]).then_inc(act2, 1)

                    biased(K2, 1, K2_FILL, 1)
                    act.wait_ge(proj2, 5 * b + 3)
                    nc.scalar.activation(X1T[:].rearrange("p m t -> p (m t)"), misc[:, XT_FILL % 2, :],
                                         ACT.Copy).then_inc(act2, 1)
                    biased(Q2, 0, Q2_FILL, 4)
                    act.wait_ge(max2, 3 * b + 3)
                    for q, (lo, hi) in enumerate(((0, 128), (128, 384))):
                        nc.scalar.activation(P2[:].rearrange("p c k -> p (c k)")[:, lo:hi],
                                             misc[:, S2_FILL % 2, lo:hi], ACT.Exp,
                                             bias=bias2[:, q:q + 1], scale=1.0 / 16.0,
                                             accum_out=sum2[:, q:q + 1]).then_inc(act2, 1)

            steps(act, run)

        @block.vector
        def _(dve):
            dve.wait_ge(weights_in, 16 * 18)
            dve.wait_ge(pool_ready, 8)
            cst = lambda n, lo=0, hi=P: CST[lo:hi, CONST_COLS[n][0]:CONST_COLS[n][1]]
            nc.vector.tensor_copy(identb[:], ident).then_inc(const_ready, 1)
            for n in masks:
                nc.vector.tensor_copy(masks[n][:], cst(n)).then_inc(const_ready, 1)
            nc.vector.tensor_copy(K1[MROW:P, :, :].rearrange("p h t -> p (h t)"), cst("pick1", MROW, P))\
                .then_inc(const_ready, 1)
            nc.vector.tensor_copy(K3[MROW:P, 0, :, :].rearrange("p h t -> p (h t)"), cst("pick3", MROW, P))\
                .then_inc(const_ready, 1)

            def norm(i, y, s, base, n):
                for q in range(2):
                    nc.vector.bn_stats(stats[:, i, q, :], y[:, q, :]).then_inc(s, 1)
                dve.wait_ge(s, base + n + 2)
                nc.vector.memset(fence[:], 0.0)
                for q in range(2):
                    nc.vector.bn_aggr(mv[:, i, q, :], stats[:, i, q, :]).then_inc(s, 1)
                dve.wait_ge(s, base + n + 4)
                nc.vector.tensor_scalar(vare[:, i, :], mv[:, i, :, 1], EPS, None, ALU.add).then_inc(s, 1)

            def norm_end(i, y, dst, s, base, n, seq):
                dve.wait_ge(rstd_ready[i], seq + 1)
                for q in range(2):
                    nc.vector.tensor_scalar(dst[:, q, :], y[:, q, :], mv[:, i, q, 0:1], rstd[:, i, q:q + 1],
                                            ALU.subtract, ALU.mult).then_inc(s, 1)
                dve.wait_ge(s, base + n + 7)

            def split_max(nmax, nmaxp, heads, maxes, n_max, split, base):
                dve.wait_ge(maxes, n_max)
                nc.vector.tensor_copy(nmaxp[:, :, 0:heads], nmax[:]).then_inc(split, 1)
                dve.wait_ge(split, base + 1)
                nc.vector.tensor_tensor(nmaxp[:, :, heads:2 * heads], nmax[:], nmaxp[:, :, 0:heads],
                                        ALU.subtract).then_inc(split, 1)

            def spread_max(mrow, dst, heads, fill, ready, n, copied, base):
                dve.wait_ge(ready, n)
                nc.vector.tensor_copy(mrow[MROW:P, :], misc[MROW:P, fill % 2, :].bitcast(BF16)[:, 0:S])\
                    .then_inc(copied, 1)
                dve.wait_ge(copied, base + 1)
                nc.vector.tensor_copy(dst, mrow[MROW:P, :].unsqueeze(1).broadcast_to([32, heads, S]))\
                    .then_inc(copied, 1)

            def run(t):
                if on("A", t):
                    a = t - LAG["A"]
                    for j in range(N_SC1):
                        dve.wait_ge(scores1, N_SC1 * a + j + 1)
                        heads, q, h = (4, 0, 4 * j) if j < 4 else (2, 1, 2 * (j - 4))
                        nc.vector.tensor_reduce(nmax1[:, q, h:h + heads],
                                                row_ps[:, j % 2, :].rearrange("p (h k) -> p h k", h=heads),
                                                AX.X, ALU.max, negate=True).then_inc(max1, 1)
                    split_max(nmax1, nmaxp1, H1, max1, N_SC1 * a + N_SC1, msplit1, 2 * a)
                if on("A", t):
                    spread_max(mrow1, Q1[MROW:P, :, :], H1, M1_FILL, mrows1, a + 1, mcopy1, 2 * a)
                if on("C", t):
                    c = t - LAG["C"]
                    for j in range(N_SC3):
                        dve.wait_ge(scores3, N_SC3 * c + j + 1)
                        dst = nmax3[:, 0, 2 * j:2 * j + 2] if j < 4 else nmax3[:, 1, 0:2]
                        nc.vector.tensor_reduce(dst, row_ps[:, j % 2, :].rearrange("p (h k) -> p h k", h=2),
                                                AX.X, ALU.max, negate=True).then_inc(max3, 1)
                    split_max(nmax3, nmaxp3, H3, max3, N_SC3 * c + N_SC3, msplit3, 2 * c)
                if on("P", t):
                    for i in range(2):
                        dve.wait_ge(high1, 2 * t + i + 1)
                        nc.vector.tensor_tensor(rest1[:, i, :], misc[:, (PQ_FILL + i) % 2, :],
                                                parts1[:, i, 0, :, :].rearrange("p m t -> p (m t)"),
                                                ALU.subtract).then_inc(evac1, 1)
                if on("C", t):
                    spread_max(mrow3, Q3[MROW:P, 0, :, :], H3, M3_FILL, mrows3, c + 1, mcopy3, 2 * c)
                if on("B3", t):
                    b = t - LAG["B3"]
                    dve.wait_ge(act2, N_ACT2 * b + 7)
                    nc.vector.reciprocal(rsum2[:], sum2[:]).then_inc(rec2, 1)
                    dve.wait_ge(rec2, b + 1)
                    dve.wait_ge(attn2, 2 * b + 2)
                    for q in range(2):
                        nc.vector.scalar_tensor_tensor(out=Y2[:, q, :], in0=misc[:, Y2_FILL % 2, q * D:q * D + D],
                                                       scalar=rsum2[:, q:q + 1], in1=X1[:, q, :],
                                                       op0=ALU.mult, op1=ALU.add).then_inc(ln2, 1)
                if on("C", t):
                    dve.wait_ge(pv3, c + 1)
                    for rows, k, t0, t1 in NESTED:
                        nc.vector.reciprocal(rsum3[0:rows, k, t0:t1], acc[0:rows, k, 1, t0:t1]).then_inc(norm3, 1)
                    dve.wait_ge(norm3, 8 * c + 4)
                    for rows, k, t0, t1 in NESTED:
                        nc.vector.tensor_tensor(OT3[0:rows, k, t0:t1], acc[0:rows, k, 0, t0:t1],
                                                rsum3[0:rows, k, t0:t1], ALU.mult).then_inc(norm3, 1)
                if on("B3", t):
                    dve.wait_ge(ln2, N_LN2 * b + 2)
                    norm(1, Y2, ln2, N_LN2 * b, 2)
                    norm_end(1, Y2, X2, ln2, N_LN2 * b, 2, b)
                    norm(2, X2, ln2b, N_LN2B * b, 0)
                    norm_end(2, X2, Z2, ln2b, N_LN2B * b, 0, b)
                if on("A", t):
                    for half in range(2):
                        dve.wait_ge(pv1, 4 * a + 2 * half + 2)
                        nc.vector.reciprocal(rsum1[:, half, :], acc[:, half, 1, :]).then_inc(norm1, 1)
                        dve.wait_ge(norm1, 4 * a + 2 * half + 1)
                        nc.vector.tensor_tensor(OT1[:, half, :], acc[:, half, 0, :], rsum1[:, half, :],
                                                ALU.mult).then_inc(norm1, 1)
                if on("P", t):
                    dve.wait_ge(proj1, 3 * t + 3)
                    v = misc[:, PV_FILL % 2, :].rearrange("p (kg w u d) -> p kg w u d", kg=4, w=2, u=4)
                    dst = V1[:].rearrange("p k (g w u) e -> p (k g) w u e", g=2, w=2)
                    for w in range(2):
                        nc.vector.tensor_copy(dst[:, :, w, :, D1 * w:D1 * w + D1], v[:, :, w, :, :]).then_inc(evac1, 1)
                if on("C", t):
                    dve.wait_ge(attn3, c + 1)
                    for r0, r1, tile, f0, f1 in NESTED_OUT:
                        nc.vector.tensor_tensor(Y3[r0:r1, tile, f0:f1], misc[r0:r1, C4_FILL % 2, tile * D + f0:tile * D + f1],
                                                Y3[r0:r1, tile, f0:f1], ALU.add).then_inc(ln3, 1)
                if on("C1", t):
                    c1 = t - LAG["C1"]
                    dve.wait_ge(proj3, 4 * c1 + 1)
                    for rows, k, t0, t1 in NESTED:
                        nc.vector.tensor_scalar(XN[0:rows, k, t0:t1], misc[0:rows, Z_FILL % 2, k * S + t0:k * S + t1],
                                                B3[0:rows, 0, k:k + 1], B3[0:rows, 1, k:k + 1],
                                                ALU.mult, ALU.add).then_inc(evac3, 1)

                def rest_of(i):
                    dve.wait_ge(high3, 4 * c1 + 2 * i + 2)
                    for m in range(2):
                        nc.vector.scalar_tensor_tensor(
                            out=rest3[:, i, m * S:m * S + S], in0=misc[:, (C1_FILL + i) % 2, m * S:m * S + S],
                            scalar=B3[:, 2 + i, m:m + 1], in1=parts3[:, i, 0, m, :],
                            op0=ALU.add, op1=ALU.subtract).then_inc(evac3, 1)

                if on("A", t):
                    dve.wait_ge(attn1, a + 1)
                    dve.wait_ge(x_in, 16 * a + 16)
                    for q in range(2):
                        nc.vector.tensor_tensor(Y1[:, q, :], misc[:, A4_FILL % 2, q * D:q * D + D], XR[:, q, :],
                                                ALU.add).then_inc(ln1, 1)
                    dve.wait_ge(ln1, N_LN1 * a + 2)
                    norm(0, Y1, ln1, N_LN1 * a, 2)
                if on("C1", t):
                    rest_of(0)
                if on("A", t):
                    norm_end(0, Y1, X1, ln1, N_LN1 * a, 2, a)
                if on("C1", t):
                    rest_of(1)
                    dve.wait_ge(proj3, 4 * c1 + 4)
                    nc.vector.tensor_tensor(V3[:], misc[:, (C1_FILL + 2) % 2, :].rearrange("p (m f) -> p m f", m=2),
                                            B3v[:].unsqueeze(1).broadcast_to([P, 2, D]), ALU.add).then_inc(evac3, 1)
                if on("C", t):
                    dve.wait_ge(ln3, N_LN3 * c + 4)
                    norm(3, Y3, ln3, N_LN3 * c, 4)
                if on("B1", t):
                    b1 = t - LAG["B1"]
                    dve.wait_ge(proj2, 5 * b1 + 2)
                    nc.vector.tensor_tensor(V2[:], misc[:, V2_FILL % 2, :].rearrange("p (m f) -> p m f", m=2),
                                            B2v[:].unsqueeze(1).broadcast_to([P, 2, D]), ALU.add).then_inc(vev2, 1)
                if on("C", t):
                    wait(dve, out_stored, 16 * c)
                    norm_end(3, Y3, OUT, ln3, N_LN3 * c, 4, c)
                if on("C1", t):
                    nc.vector.scalar_tensor_tensor(out=Y3[:], in0=X2[:], scalar=2.0, in1=B3o[:],
                                                   op0=ALU.mult, op1=ALU.add).then_inc(evac3, 1)
                if on("B1", t):
                    dve.wait_ge(proj2, 5 * b1 + 5)
                    for q, (lo, hi) in enumerate(((0, 128), (128, 384))):
                        nc.vector.tensor_reduce(nmax2[:, q:q + 1], misc[:, S2_FILL % 2, lo:hi], AX.X, ALU.max,
                                                negate=True).then_inc(max2, 1)
                    dve.wait_ge(max2, 3 * b1 + 2)
                    nc.vector.tensor_scalar(bias2[:], nmax2[:], 1.0 / 16.0, None, ALU.mult).then_inc(max2, 1)

            steps(dve, run)

        @block.tensor
        def _(pe):
            mm = nc.tensor.matmul

            def tokens_by_feature(bank, w, xt, cols=None):
                for m in range(2):
                    for k in range(2):
                        n = S if cols is None or k == 0 else cols
                        last = mm(misc[:, bank, m * S:m * S + n], w[:, k, m * P:m * P + P], xt[:, k, 0:n],
                                  start=(k == 0), stop=(k == 1), skip_group_check=True)
                return last

            def features_by_token(bank, w, xt):
                for q in range(2):
                    for k in range(2):
                        last = mm(misc[:, bank, q * D:q * D + D], xt[:, k, q * P:q * P + P], w[:, k, 0:D],
                                  start=(k == 0), stop=(k == 1))
                return last

            def turn(bank, src):
                for k in range(2):
                    for q in range(2):
                        last = nc.tensor.transpose(misc[:, bank, k * S + q * P:k * S + q * P + P],
                                                   src[:, q, k * P:k * P + P], ident)
                return last

            def Z(t):
                c = t - LAG["C1"]
                pe.wait_ge(ln2b, N_LN2B * c + 7)
                misc_free(pe, t, Z_FILL)
                turn(Z_FILL % 2, Z2).then_inc(proj3, 1)

            def C1(t):
                c = t - LAG["C1"]
                pe.wait_ge(evac3, N_EV3 * c + 4)
                for i, w in enumerate((W3q, W3k)):
                    misc_free(pe, t, C1_FILL + i)
                    tokens_by_feature((C1_FILL + i) % 2, w, XN, P).then_inc(proj3, 1)
                misc_free(pe, t, C1_FILL + 2)
                bank = (C1_FILL + 2) % 2
                mm(misc[:, bank, 0:D], XN[:, 0, 0:P], W3v[:, 0, :], start=True, stop=False)
                mm(misc[:, bank, 0:D], XN[:, 1, 0:P], W3v[:, 1, :], start=False, stop=True)
                mm(misc[:, bank, D:2 * D], XN[:, 0, P:S], W3v[:, 0, :], start=True, stop=True).then_inc(proj3, 1)

            def A2(t):
                a = t - LAG["A"]
                pe.wait_ge(stacks1_in, 192 * a + 192)
                for j in range(N_SC1):
                    bank = row_ps[:, j % 2, :]
                    if j >= 2:
                        pe.wait_ge(max1, N_SC1 * a + j - 1)
                    else:
                        if not fixed(t) or t > LAG["C"]:
                            pe.wait_ge(max3, N_SC3 * (t - LAG["C"]))
                        if fixed(a):
                            wait(pe, max1, N_SC1 * a)
                    if j < 4:
                        mm(bank, identb[:], masks["mask_q0"][:], start=True, stop=False)
                        for u in range(4):
                            h = 4 * j + u
                            last = mm(bank[:, u * P:u * P + P], Q1[0:MROW, h, 0:P], K1[0:MROW, h, 0:P],
                                      start=False, stop=(u == 3))
                    else:
                        mm(bank, identb[:], masks["mask_q1"][:], start=True, stop=False)
                        for u in range(2):
                            h = 2 * (j - 4) + u
                            last = mm(bank[:, u * S:u * S + S], Q1[0:MROW, h, P:S], K1[0:MROW, h, :],
                                      start=False, stop=(u == 1))
                    last.then_inc(scores1, 1)

            def B1(t):
                b = t - LAG["B1"]
                pe.wait_ge(ctxT_in, 16 * b + 16)
                misc_free(pe, t, K2_FILL)
                tokens_by_feature(K2_FILL % 2, W2k, CT).then_inc(proj2, 1)
                misc_free(pe, t, V2_FILL)
                features_by_token(V2_FILL % 2, W2v, CT).then_inc(proj2, 1)
                pe.wait_ge(ln1, N_LN1 * b + N_LN1)
                misc_free(pe, t, XT_FILL)
                turn(XT_FILL % 2, X1).then_inc(proj2, 1)
                pe.wait_ge(act2, N_ACT2 * b + 3)
                misc_free(pe, t, Q2_FILL)
                tokens_by_feature(Q2_FILL % 2, W2q, X1T).then_inc(proj2, 1)
                pe.wait_ge(act2, N_ACT2 * b + 5)
                misc_free(pe, t, S2_FILL)
                bank = misc[:, S2_FILL % 2, :]
                mm(bank[:, 0:P], identb[:], masks["mask_q0"][:, 0:P], start=True, stop=False)
                for k in range(2):
                    mm(bank[:, 0:P], Q2[:, k, 0:P], K2[:, k, 0:P], start=False, stop=(k == 1))
                mm(bank[:, S:S + P], identb[:], masks["mask_q0"][:, 0:P], start=True, stop=False,
                   skip_group_check=True)
                for k in range(2):
                    last = mm(bank[:, P:P + S], Q2[:, k, P:S], K2[:, k, :], start=False, stop=(k == 1),
                              skip_group_check=True)
                last.then_inc(proj2, 1)

            def turn_max(t, stage, fill, split, nmaxp, ready):
                n = t - LAG[stage]
                misc_free(pe, t, fill)
                pe.wait_ge(split, 2 * n + 2)
                rows = misc[MROW:P, fill % 2, :].bitcast(BF16)
                for q in range(2):
                    last = nc.tensor.transpose(rows[:, q * P:q * P + P], nmaxp[:, q, :], identb[:])
                last.then_inc(ready, 1)

            def A3(t):
                a = t - LAG["A"]
                def scores(g, f):
                    j = 3 * g + f
                    bank = col_ps[:, j % 2, :]
                    if j == 0:
                        pe.wait_ge(mcopy1, 2 * a + 2)
                    if j >= 2:
                        pe.wait_ge(exp1, N_T1 * a + j - 1)
                    else:
                        if not fixed(t) or t >= LAG["C"]:
                            pe.wait_ge(exp3, N_T3 * (t - LAG["C"] + 1))
                        if fixed(a):
                            wait(pe, exp1, N_T1 * a)
                    mm(bank, identb[:], masks["mask_k1" if f == 2 else "mask_k0"][:], start=True, stop=False)
                    if f < 2:
                        for u in range(2):
                            h = 4 * g + 2 * f + u
                            last = mm(bank[:, u * S:u * S + S], K1[:, h, 0:P], Q1[:, h, :], start=False, stop=(u == 1))
                    else:
                        for u in range(4):
                            h = 4 * g + u
                            last = mm(bank[:, u * P:u * P + P], K1[:, h, P:S], Q1[:, h, P:S], start=False, stop=(u == 3))
                    last.then_inc(scoresT1, 1)

                def products(g, f):
                    p = PT1[:, g % 2, :, :]
                    even = g % 2 == 0
                    ones = ones_lo if even else ones_hi
                    bank = acc[:, g // 2, :, :]
                    if g == 0 and f == 0:
                        if not fixed(t) or t >= LAG["C"]:
                            pe.wait_ge(norm3, 8 * (t - LAG["C"] + 1))
                        if fixed(a):
                            wait(pe, norm1, 4 * a)
                    if f < 2:
                        pe.wait_ge(exp1, N_T1 * a + 3 * g + 2)
                        for u in range(4):
                            w = V1[:, 0, 4 * g + u, :] if f == 0 else ones
                            last = mm(bank[32 * u:32 * u + 32, f, :], w, p[:, u // 2, (u % 2) * S:(u % 2) * S + S],
                                      start=(even and f == 0), stop=False, skip_group_check=True)
                    else:
                        pe.wait_ge(exp1, N_T1 * a + 3 * g + 3)
                        for i in range(2):
                            for u in range(4):
                                w = V1[:, 1, 4 * g + u, :] if i == 0 else ones
                                last = mm(bank[32 * u:32 * u + 32, i, P:S], w, p[:, 2, u * P:u * P + P],
                                          start=False, stop=not even, skip_group_check=True)
                        last.then_inc(pv1, 1)

                for g in range(5):
                    for f in range(3):
                        if g < 4:
                            scores(g, f)
                        if g > 0:
                            products(g - 1, f)

            def B3p(t):
                b = t - LAG["B3"]
                pe.wait_ge(act2, N_ACT2 * b + 7)
                misc_free(pe, t, PT2_FILL)
                for i in range(3):
                    last = nc.tensor.transpose(misc[:, PT2_FILL % 2, i * P:i * P + P], P2[:, i, :], ident)
                last.then_inc(attn2, 1)
                misc_free(pe, t, Y2_FILL)
                pe.wait_ge(pT2, b + 1)
                bank = Y2_FILL % 2
                mm(misc[:, bank, 0:D], PT2[:, 0, :], V2[:, 0, :], start=True, stop=True)
                mm(misc[:, bank, D:2 * D], PT2[:, 1, :], V2[:, 0, :], start=True, stop=False)
                mm(misc[:, bank, D:2 * D], PT2[:, 2, :], V2[:, 1, :], start=False, stop=True).then_inc(attn2, 1)

            def C2(t):
                c = t - LAG["C"]
                pe.wait_ge(stacks3_in, 192 * c + 192)
                for j in range(N_SC3):
                    if j >= 2:
                        pe.wait_ge(max3, N_SC3 * c + j - 1)
                    else:
                        a = min(t - LAG["A"], NB - 1) if fixed(t) else t - LAG["A"]
                        pe.wait_ge(max1, N_SC1 * (a + 1))
                        if fixed(c):
                            wait(pe, max3, N_SC3 * c)
                    q, h0 = (0, 2 * j) if j < 4 else (1, 0)
                    for u in range(2):
                        for s in range(2):
                            last = mm(row_ps[:, j % 2, u * S:u * S + S], Q3[0:MROW, s, h0 + u, q * P:q * P + P],
                                      K3[0:MROW, s, h0 + u, :], start=(s == 0), stop=(s == 1))
                    last.then_inc(scores3, 1)

            def P_qk(t):
                pe.wait_ge(xT_in, 16 * t + 16)
                for i in range(2):
                    misc_free(pe, t, PQ_FILL + i)
                    tokens_by_feature((PQ_FILL + i) % 2, W1[:, :, i * D:i * D + D], XT).then_inc(proj1, 1)

            def P_v(t):
                misc_free(pe, t, PV_FILL)
                features_by_token(PV_FILL % 2, W1[:, :, 2 * D:3 * D], XT).then_inc(proj1, 1)

            def C3(t):
                c = t - LAG["C"]
                a = min(t - LAG["A"], NB) if fixed(t) else t - LAG["A"]
                pe.wait_ge(mcopy3, 2 * c + 2)
                for j in range(N_T3):
                    if j >= 2:
                        pe.wait_ge(exp3, N_T3 * c + j - 1)
                    else:
                        pe.wait_ge(exp1, N_T1 * a)
                        if fixed(c):
                            wait(pe, exp3, N_T3 * c)
                    keys = slice((j // 2) * P, (j // 2) * P + P)
                    for h, col in T3_BANKS[j % 2]:
                        n = Q3_USED[h]
                        for s, rows_used in ((0, P), (1, MROW)):
                            last = mm(col_ps[:, j % 2, col:col + n], K3[0:rows_used, s, h, keys],
                                      Q3[0:rows_used, s, h, 0:n], start=(s == 0), stop=(s == 1))
                    last.then_inc(scoresT3, 1)
                pe.wait_ge(norm1, 4 * a)
                if fixed(c):
                    wait(pe, norm3, 8 * c)
                place = {h: (f, col) for f in range(2) for h, col in T3_BANKS[f]}
                for k in range(2):
                    pe.wait_ge(exp3, N_T3 * c + 2 * k + 2)
                    for half in range(2):
                        for i in range(2):
                            for u in range(4):
                                h = 4 * half + u
                                f, col = place[h]
                                n = Q3_USED[h]
                                w = V3[:, k, D3 * h:D3 * h + D3] if i == 0 else ones32[:]
                                last = mm(acc[32 * u:32 * u + 32, half, i, 0:n], w, PT3[:, k, f, col:col + n],
                                          start=(k == 0 and i == 0), stop=(k == 1), skip_group_check=True)
                last.then_inc(pv3, 1)

            def A4(t):
                a = t - LAG["A"]
                pe.wait_ge(norm1, 4 * a + 4)
                misc_free(pe, t, A4_FILL)
                features_by_token(A4_FILL % 2, W1o, OT1).then_inc(attn1, 1)

            def C4(t):
                c = t - LAG["C"]
                pe.wait_ge(norm3, 8 * c + 8)
                misc_free(pe, t, C4_FILL)
                bank = C4_FILL % 2
                mm(misc[:, bank, 0:D], OT3[:, 0, 0:P], W3o[:, 0, :], start=True, stop=False)
                mm(misc[:, bank, 0:D], OT3[:, 1, 0:P], W3o[:, 1, :], start=False, stop=True)
                mm(misc[:, bank, D:D + P], OT3[:, 0, P:S], W3o[:, 0, 0:P], start=True, stop=True).then_inc(attn3, 1)

            def run(t):
                for stage, phase in (
                        ("A", A2), ("A", lambda t: turn_max(t, "A", M1_FILL, msplit1, nmaxp1, mrows1)),
                        ("C", C2), ("P", P_qk), ("C", lambda t: turn_max(t, "C", M3_FILL, msplit3, nmaxp3, mrows3)),
                        ("B3", B3p), ("C", C3), ("A", A3), ("P", P_v), ("C", C4), ("C1", Z), ("A", A4),
                        ("C1", C1), ("B1", B1)):
                    if on(stage, t):
                        phase(t)

            pe.wait_ge(weights_in, 16 * 18)
            pe.wait_ge(const_ready, 7)
            steps(pe, run)


def layer_constants():
    import numpy as np
    c = np.zeros((P, CONST_W), np.float32)

    def put(name, a, rows=slice(None)):
        c[rows, CONST_COLS[name][0]:CONST_COLS[name][1]] = a

    i, j = np.arange(P)[:, None], np.arange(P)[None, :]
    causal = np.where(j <= i, 0.0, NEG)
    band = np.where((j > i) | (j < PREFIX), 0.0, NEG)
    put("ident", np.eye(P))
    put("mask_q0", np.tile(causal, (1, 4)))
    put("mask_q1", np.tile(np.concatenate([band, causal], 1), (1, 2)))
    put("mask_k0", np.tile(np.concatenate([causal.T, band.T], 1), (1, 2)))
    put("mask_k1", np.tile(causal.T, (1, 4)))
    ones = np.zeros((P, 64))
    ones[:, 0:D1] = 1.0
    ones[:, 32 + D1:64] = 1.0
    put("ones", ones)
    for name, heads in (("pick1", H1), ("pick3", H3)):
        pick = np.zeros((32, heads, S))
        for h in range(heads):
            pick[[h, heads + h], h, :] = 1.0
        put(name, pick.reshape(32, heads * S), slice(MROW, P))
    return c


def kernel(**inputs):
    import numpy as np
    import concourse.bacc as bacc
    from concourse.bass_utils import run_bass_kernel_spmd

    g = {k: np.asarray(v) for k, v in inputs.items()}
    nc = bacc.Bacc("TRN2", target_bir_lowering=False, num_devices=1)

    def by_feature(a):
        return a.reshape(NB * S, 2, P).transpose(2, 1, 0)

    def by_token(a):
        return a.reshape(NB * 2, P, D).transpose(1, 0, 2)

    def halves(*vs):
        return np.stack([v.reshape(2, P) for v in vs]).transpose(2, 0, 1)

    w_out = g["L0_attn_w_out"].T.reshape(2, 2, 4, D1, D).transpose(0, 2, 1, 3, 4).reshape(D, D)
    arrays = {
        "xT": by_feature(g["x"]), "x": by_token(g["x"]), "ctxT": by_feature(g["ctx_1024"]),
        "consts": layer_constants(),
        "w1_qkvT": g["L0_attn_w_qkv"].T, "w1_oT": w_out,
        "w2_qT": g["L0_xattn_wq_w"].T, "w2_kT": g["L0_xattn_wk_w"].T, "w2_vT": g["L0_xattn_wv_w"].T,
        "b2": halves(g["L0_xattn_wq_b"], g["L0_xattn_wk_b"]), "bv2": g["L0_xattn_wv_b"],
        "w3_qT": g["L0_ffn_q_w"].T, "w3_kT": g["L0_ffn_k_w"].T, "w3_vT": g["L0_ffn_v_w"].T,
        "w3_oT": g["L0_ffn_o_w"].T,
        "b3": halves(g["L0_ffn_norm_w"], g["L0_ffn_norm_b"], g["L0_ffn_q_b"], g["L0_ffn_k_b"]),
        "bv3": g["L0_ffn_v_b"], "bo3": g["L0_ffn_o_b"],
    }
    arrays = {k: np.ascontiguousarray(v) for k, v in arrays.items()}
    args = [nc.dram_tensor(f"in_{k}", v.shape, mybir.dt.from_np(v.dtype), kind="ExternalInput").ap()
            for k, v in arrays.items()]
    out = nc.dram_tensor("out", (P, NB * 2, D), F32, kind="ExternalOutput").ap()
    build(nc, *args, out)
    r = run_bass_kernel_spmd(nc, [{f"in_{k}": v for k, v in arrays.items()}], core_ids=[0])
    got = np.asarray(r.results[0]["out"])
    return got.transpose(1, 0, 2).reshape(NB, S, D)
```

```python
from contextlib import ExitStack

import concourse.bass as bass
from concourse import mybir

F32 = mybir.dt.float32
BF16 = mybir.dt.bfloat16
ALU = mybir.AluOpType
ACT = mybir.ActivationFunctionType
AX = mybir.AxisListType

NB, S, D = 16, 256, 256
P = 128
H1, D1 = 16, D // 16
H3, D3 = 8, D // 8
PREFIX = 16
EPS = 1e-5
NEG = -1.0e30

Q1_PARTS, K1_PARTS = (0, 0, 1, 1, 0, 2), (0, 1, 0, 1, 2, 0)
Q3_PARTS, K3_PARTS = ((0, 0, 1), (1, 0, 2)), ((0, 1, 0), (1, 2, 0))
MROW = 96

NESTED = ((128, 0, 0, 128), (64, 0, 128, 192), (32, 0, 192, 256), (128, 1, 0, 64))
NESTED_OUT = ((0, 128, 0, 0, 128), (0, 64, 0, 128, 256), (0, 64, 1, 0, 64), (64, 128, 1, 0, 32))
Q3_USED = (256, 192, 128, 128, 64, 64, 64, 64)
T3_BANKS = (((0, 0), (1, 256), (4, 448)), ((2, 0), (3, 128), (5, 256), (6, 320), (7, 384)))
T3_COLS = (512, 448)

LAG = {"P": 0, "A": 1, "B": 2, "C1": 2, "C": 3}

CONST_COLS = {}
_at = 0
for _name, _n in (("ident", 128), ("band", 128), ("causal", 128), ("bandT", 128),
                  ("ones", 64), ("pick1", H1), ("pick3", H3)):
    CONST_COLS[_name] = (_at, _at + _n)
    _at += _n
CONST_W = _at


def build(nc, xT, x, ctxT, consts, w1_qkvT, w1_oT, w2_qT, w2_kT, w2_vT, b2, bv2, w3_qT, w3_kT, w3_vT,
          w3_oT, b3, bv3, bo3, out):
    with ExitStack() as ctx:
        def sb(name, shape, dt=F32):
            return ctx.enter_context(nc.sbuf_tensor(name, shape, dt))

        def psum(name, shape):
            return ctx.enter_context(nc.psum_tensor(name, shape, F32))

        def sem(name):
            return ctx.enter_context(nc.semaphore(name))

        parts1_dram = nc.dram_tensor("parts1_dram", [6, D, S], BF16, kind="Internal").ap()
        parts3_dram = nc.dram_tensor("parts3_dram", [6, D, S], BF16, kind="Internal").ap()

        W1 = sb("W1", [P, 2, 3 * D])
        W1o = sb("W1o", [P, 2, D])
        W2q, W2k, W2v = sb("W2q", [P, 2, D]), sb("W2k", [P, 2, D]), sb("W2v", [P, 2, D])
        W3q, W3k, W3v, W3o = (sb(n, [P, 2, D]) for n in ("W3q", "W3k", "W3v", "W3o"))
        B2 = sb("B2", [P, 2, 2])
        B2v = sb("B2v", [P, D])
        B3 = sb("B3", [P, 4, 2])
        B3v = sb("B3v", [P, D])
        B3o = sb("B3o", [P, 2, D])
        CST = sb("CST", [P, CONST_W])
        ident = CST[:, CONST_COLS["ident"][0]:CONST_COLS["ident"][1]]
        identb = sb("identb", [P, P], BF16)
        MASKS = {"mask_q0": ("causal",) * 4, "mask_k0": ("bandT",) * 2}
        masks = {n: sb(n, [P, P * len(MASKS[n])], BF16) for n in MASKS}
        mask_last = CST[:, CONST_COLS["band"][0]:CONST_COLS["causal"][1]]
        ones_lo = CST[:, CONST_COLS["ones"][0]:CONST_COLS["ones"][0] + 32]
        ones_hi = CST[:, CONST_COLS["ones"][0] + 32:CONST_COLS["ones"][1]]
        ones32 = sb("ones32", [P, 32])
        minus_half = sb("minus_half", [P, 2])

        XT = sb("XT", [P, 2, S])
        XR = sb("XR", [P, 2, D])
        parts1 = sb("parts1", [P, 2, 3, 2, S], BF16)
        rest1 = sb("rest1", [P, 2, 2 * S])
        V1 = sb("V1", [P, 2, H1, 32])
        Q1, K1 = sb("Q1", [P, 2, H1, S], BF16), sb("K1", [P, 2, H1, S], BF16)
        nmax1 = sb("nmax1", [P, 2, H1])
        unused = sb("unused", [P, H1, S])
        nmaxp1 = sb("nmaxp1", [P, 2, 32], BF16)
        mrow1 = sb("mrow1", [P, S], BF16)
        PT1 = sb("PT1", [P, 2, 3, 512])
        rsum1 = sb("rsum1", [P, 2, S])
        OT1 = sb("OT1", [P, 2, S])
        Y1, X1 = sb("Y1", [P, 2, D]), sb("X1", [P, 2, D])
        CT = sb("CT", [P, 2, S])
        X1T, Q2, K2 = sb("X1T", [P, 2, S]), sb("Q2", [P, 2, S]), sb("K2", [P, 2, S])
        V2 = sb("V2", [P, 2, D])
        X1b = sb("X1b", [P, 2, D])
        nmax2, bias2 = sb("nmax2", [P, 2]), sb("bias2", [P, 2])
        sum2, rsum2 = sb("sum2", [P, 2]), sb("rsum2", [P, 2])
        P2, PT2 = sb("P2", [P, 3, P]), sb("PT2", [P, 3, P])
        Y2, X2, Z2 = sb("Y2", [P, 2, D]), sb("X2", [P, 2, D]), sb("Z2", [P, 2, D])
        XN = sb("XN", [P, 2, S])
        parts3 = sb("parts3", [P, 2, 3, 2, S], BF16)
        rest3 = sb("rest3", [P, 2, 2 * S])
        V3_plain, V3 = sb("V3_plain", [P, 2, D]), sb("V3", [P, 2, D])
        Q3, K3 = sb("Q3", [P, 2, 2, H3, S], BF16), sb("K3", [P, 2, 2, H3, S], BF16)
        nmax3 = sb("nmax3", [P, 2, H3])
        nmaxp3 = sb("nmaxp3", [P, 2, 32], BF16)
        mrow3 = sb("mrow3", [P, S], BF16)
        PT3 = sb("PT3", [P, 2, 2, 512])
        rsum3 = sb("rsum3", [P, 2, S])
        OT3 = sb("OT3", [P, 2, S])
        Y3, OUT = sb("Y3", [P, 2, D]), sb("OUT", [P, 2, D])
        stats = sb("stats", [P, 4, 2, 6])
        mv = sb("mv", [P, 4, 2, 2])
        vare = sb("vare", [P, 4, 2])
        rstd = sb("rstd", [P, 4, 2])
        nmean, shift = sb("nmean", [P, 4, 2]), sb("shift", [P, 4, 2])
        fence, pool_fence = sb("fence", [P, 16]), sb("pool_fence", [P, 12])

        row_ps = psum("row_ps", [P, 2, 512])
        col_ps = psum("col_ps", [P, 2, 512])
        acc = psum("acc", [P, 2, 2, S])
        misc = psum("misc", [P, 2, 512])

        w1_in, w1v_in, consts_in, weights_in, weights3_in = (
            sem(n) for n in ("w1_in", "w1v_in", "consts_in", "weights_in", "weights3_in"))
        xT_in, x_in, ctxT_in = sem("xT_in"), sem("x_in"), sem("ctxT_in")
        q_out1, k_out1, q_out3, k_out3 = (sem(n) for n in ("q_out1", "k_out1", "q_out3", "k_out3"))
        stacks1_in, stacks3_in = sem("stacks1_in"), sem("stacks3_in")
        out_stored = sem("out_stored")
        const_ready, pool_ready = sem("const_ready"), sem("pool_ready")
        proj1, scores1, mrows1, scoresT1, pv1, attn1 = (
            sem(n) for n in ("proj1", "scores1", "mrows1", "scoresT1", "pv1", "attn1"))
        proj2, attn2 = sem("proj2"), sem("attn2")
        proj3, scores3, mrows3, scoresT3, pv3, attn3 = (
            sem(n) for n in ("proj3", "scores3", "mrows3", "scoresT3", "pv3", "attn3"))
        high1, mid1, exp1 = sem("high1"), sem("mid1"), sem("exp1")
        act2, pT2 = sem("act2"), sem("pT2")
        v1_ready, v2_ready, xn_ready = sem("v1_ready"), sem("v2_ready"), sem("xn_ready")
        v3_plain, v3_ready = sem("v3_plain"), sem("v3_ready")
        x1_ready, x2_ready, z2_ready, out_ready = (
            sem(n) for n in ("x1_ready", "x2_ready", "z2_ready", "out_ready"))
        high3, mid3, exp3 = sem("high3"), sem("mid3"), sem("exp3")
        low1, low3, y3_ready, select1, x1b_ready = (
            sem(n) for n in ("low1", "low3", "y3_ready", "select1", "x1b_ready"))
        rstd_ready = [sem(f"rstd_ready{i}") for i in range(4)]
        evac1, max1, msplit1, mcopy1, norm1, ln1 = (
            sem(n) for n in ("evac1", "max1", "msplit1", "mcopy1", "norm1", "ln1"))
        rec2, max2, ln2, ln2b = sem("rec2"), sem("max2"), sem("ln2"), sem("ln2b")
        evac3, max3, msplit3, mcopy3, norm3, ln3 = (
            sem(n) for n in ("evac3", "max3", "msplit3", "mcopy3", "norm3", "ln3"))

        N_EV1, N_EV3, N_ACT2, N_LN1, N_LN2, N_LN2B, N_LN3 = 2, 4, 7, 8, 8, 6, 10
        N_SC1, N_SC3, N_T1, N_T3 = 12, 5, 12, 4

        FILLS = {"A2_0": ("r0", "A", max1, N_SC1, N_SC1 - 1), "A2_1": ("r1", "A", max1, N_SC1, N_SC1),
                 "K2": ("m0", "B", act2, N_ACT2, 2), "V2": ("m1", "B", v2_ready, 1, 1),
                 "X1T": ("m0", "B", act2, N_ACT2, 3), "Q2": ("m0", "B", act2, N_ACT2, 5),
                 "C2_0": ("r0", "C", max3, N_SC3, N_SC3), "C2_1": ("r1", "C", max3, N_SC3, N_SC3 - 1),
                 "Pq": ("m1", "P", evac1, N_EV1, 1), "S2": ("m0", "B", act2, N_ACT2, 7),
                 "mT1": ("r0", "A", mcopy1, 2, 1), "Pk": ("r1", "P", evac1, N_EV1, 2),
                 "mT3": ("r0", "C", mcopy3, 2, 1), "PT2": ("m0", "B", pT2, 1, 1),
                 "Y2": ("r0", "B", ln2, N_LN2, 2), "Pv": ("r1", "P", v1_ready, 2, 2),
                 "C4": ("r0", "C", ln3, N_LN3, 4), "Z": ("m0", "C1", xn_ready, 4, 4),
                 "C1q": ("m1", "C1", evac3, N_EV3, 2), "C1k": ("r0", "C1", evac3, N_EV3, 4),
                 "A4": ("m0", "A", ln1, N_LN1, 2), "C1v": ("m1", "C1", v3_plain, 1, 1)}
        BANKS = {"m0": misc[:, 0, :], "m1": misc[:, 1, :], "r0": row_ps[:, 0, :], "r1": row_ps[:, 1, :]}

        def bank_of(fill):
            return BANKS[FILLS[fill][0]]

        def fixed(t):
            return type(t) is int

        def on(stage, t):
            return not fixed(t) or 0 <= t - LAG[stage] < NB

        def wait(eng, s, n):
            if not fixed(n) or n > 0:
                eng.wait_ge(s, n)

        def bank_free(pe, t, fill):
            order = list(FILLS)
            n = order.index(fill)
            same = [m for m in range(len(order)) if FILLS[order[m]][0] == FILLS[fill][0]]
            if not fixed(t):
                m = same[same.index(n) - 1]
                _, stage, s, per, after = FILLS[order[m]]
                pe.wait_ge(s, (t - LAG[stage] - (0 if m < n else 1)) * per + after)
                return
            for m in same:
                _, stage, s, per, after = FILLS[order[m]]
                seq = min(t - LAG[stage] - (0 if m < n else 1), NB - 1)
                if seq >= 0:
                    pe.wait_ge(s, seq * per + after)

        def steps(eng, run):
            for t in range(4):
                run(t, t % 2)
            with eng.Fori(4, NB - 3, 2) as t:
                run(t, 0)
                run(t + 1, 1)
            for t in range(NB - 2, NB + LAG["C"]):
                run(t, t % 2)

        def wait_weights(eng, t):
            if fixed(t) and t == 1:
                eng.wait_ge(weights_in, 16 * 6)
            if fixed(t) and t == 2:
                eng.wait_ge(weights3_in, 16 * 10)

        block = ctx.enter_context(nc.Block())

        @block.sync
        def _(sp):
            n = 0

            def load(dst, src, landed):
                sp.dma_start(dst, src).then_inc(landed, 16)

            def load_weights(pairs, landed):
                for dst, src in pairs:
                    load(dst[:], src.rearrange("(k p) o -> p k o", p=P), landed)

            w1 = w1_qkvT.rearrange("(k p) o -> p k o", p=P)
            load(W1[:, :, 0:2 * D], w1[:, :, 0:2 * D], w1_in)
            load(XT[:], xT[:, :, 0:S], xT_in)
            load(W1[:, :, 2 * D:3 * D], w1[:, :, 2 * D:3 * D], w1v_in)
            load(CST[:], consts, consts_in)
            load_weights(((W1o, w1_oT), (W2k, w2_kT), (W2q, w2_qT), (W2v, w2_vT)), weights_in)
            load(B2[:], b2, weights_in)
            load(B2v[:], bv2.partition_broadcast(P), weights_in)

            def load_weights3():
                load_weights(((W3q, w3_qT), (W3k, w3_kT), (W3v, w3_vT), (W3o, w3_oT)), weights3_in)
                load(B3[:], b3, weights3_in)
                load(B3v[:], bv3.partition_broadcast(P), weights3_in)
                sp.wait_ge(pool_ready, 8)
                for r0, r1, tile, f0, f1 in NESTED_OUT:
                    load(B3o[r0:r1, tile, f0:f1], bo3[f0:f1].partition_broadcast(r1 - r0), weights3_in)

            def run(t, odd):
                p, a, b, c1, c = (t - LAG[x] for x in ("P", "A", "B", "C1", "C"))

                def count(n):
                    return n if fixed(n) else sp.snap(n)

                def bounce_out(scratch, parts, i, wrote):
                    sp.dma_start(scratch[3 * i:3 * i + 3].rearrange("s (m p) t -> p s m t", p=P),
                                 parts[:, i, :, :, :]).then_inc(wrote, 16)

                def stack(dst, scratch, which, width, landed):
                    for r, part in enumerate(which):
                        sp.dma_start(dst[width * r:width * r + width, :, :], scratch[part].rearrange(
                            "(h d) t -> d h t", d=width)).then_inc(landed, 16)

                if on("A", t):
                    wait(sp, ln1, count((a - 1) * N_LN1 + 2))
                    sp.dma_start(XR[:], x[:, bass.ds(count(a * 2), 2), :]).then_inc(x_in, 16)
                if on("P", t):
                    wait(sp, stacks1_in, count(192 * p))
                    sp.wait_ge(low1, count(2 * p + 1))
                    bounce_out(parts1_dram, parts1, 0, q_out1)
                    sp.wait_ge(low1, count(2 * p + 2))
                    bounce_out(parts1_dram, parts1, 1, k_out1)
                    sp.wait_ge(q_out1, count(16 * p + 16))
                    stack(Q1[:, odd], parts1_dram, Q1_PARTS, D1, stacks1_in)
                    sp.wait_ge(k_out1, count(16 * p + 16))
                    stack(K1[:, odd], parts1_dram, [3 + x for x in K1_PARTS], D1, stacks1_in)
                if fixed(t) and t == 0:
                    load_weights3()
                if on("A", t):
                    wait(sp, proj2, count(5 * a))
                if not fixed(t) or t + 1 < NB:
                    sp.wait_ge(proj1, count(3 * p + 3))
                    sp.dma_start(XT[:], xT[:, :, bass.ds(count(p * S + S), S)]).then_inc(xT_in, 16)
                if on("A", t):
                    sp.dma_start(CT[:], ctxT[:, :, bass.ds(count(a * S), S)]).then_inc(ctxT_in, 16)
                if on("C1", t):
                    wait(sp, pv3, count(c1))
                if on("C", t):
                    sp.wait_ge(out_ready, count(2 * c + 2))
                    sp.dma_start(out[:, bass.ds(count(c * 2), 2), :], OUT[:]).then_inc(out_stored, 16)
                if on("C1", t):
                    sp.wait_ge(low3, count(2 * c1 + 1))
                    bounce_out(parts3_dram, parts3, 0, q_out3)
                    sp.wait_ge(low3, count(2 * c1 + 2))
                    bounce_out(parts3_dram, parts3, 1, k_out3)
                    sp.wait_ge(q_out3, count(16 * c1 + 16))
                    for j in range(2):
                        stack(Q3[:, odd, j, :, :], parts3_dram, Q3_PARTS[j], D3, stacks3_in)
                    sp.wait_ge(k_out3, count(16 * c1 + 16))
                    for j in range(2):
                        stack(K3[:, odd, j, :, :], parts3_dram, [3 + x for x in K3_PARTS[j]], D3, stacks3_in)

            steps(sp, run)
            sp.wait_ge(out_stored, 16 * NB)

        @block.gpsimd
        def _(pool):
            for zeroed in (V1, XN, OT3, nmax3, nmaxp3, B3o):
                nc.gpsimd.memset(zeroed[:], 0.0).then_inc(pool_ready, 1)
            nc.gpsimd.memset(ones32[:], 1.0).then_inc(pool_ready, 1)
            nc.gpsimd.memset(minus_half[:], -0.5).then_inc(pool_ready, 1)
            pool.wait_ge(pool_ready, 8)

            def select(t, j):
                a = t - LAG["A"]
                g, f = j // 3, j % 3
                pool.wait_ge(exp1, N_T1 * a + j + 1)
                nc.gpsimd.tensor_tensor(pool_fence[:, j:j + 1], minus_half[:, 0:1], minus_half[:, 0:1], ALU.add)
                p = PT1[:, g % 2, f, :]
                if f < 2:
                    p = p.rearrange("p (u w q) -> p u w q", u=2, w=2)[:, :, 0, :]
                else:
                    p = p.rearrange("p (u q) -> p u q", u=4)
                nc.gpsimd.affine_select(p, p, [[0, 2 if f < 2 else 4], [1, P]], ALU.is_ge, fill_zero, base=0,
                                        channel_multiplier=-1).then_inc(select1, 1)

            fill_zero = pool.to_reg(0.0)

            def low_part(rest, parts, mid, low, i, n):
                pool.wait_ge(mid, n)
                nc.gpsimd.tensor_tensor(parts[:, i, 2, :, :].rearrange("p m t -> p (m t)"), rest[:, i, :],
                                        parts[:, i, 1, :, :].rearrange("p m t -> p (m t)"),
                                        ALU.subtract).then_inc(low, 1)

            def root(i, ready, n, seq):
                pool.wait_ge(ready, n)
                nc.gpsimd.tensor_tensor(rstd[:, i, :], vare[:, i, :], minus_half[:], ALU.pow)\
                    .then_inc(rstd_ready[i], 1)
                pool.wait_ge(rstd_ready[i], 2 * seq + 1)
                nc.gpsimd.tensor_tensor(shift[:, i, :], nmean[:, i, :], rstd[:, i, :], ALU.mult)\
                    .then_inc(rstd_ready[i], 1)

            def run(t, odd):
                wait_weights(pool, t)
                p, a, b, c1, c = (t - LAG[x] for x in ("P", "A", "B", "C1", "C"))
                if on("B", t):
                    root(0, ln1, N_LN1 * b + N_LN1, b)
                    pool.wait_ge(x1_ready, 2 * b + 2)
                    nc.gpsimd.tensor_tensor(X1b[:], X1[:], B2v[:].unsqueeze(1).broadcast_to([P, 2, D]), ALU.add)\
                        .then_inc(x1b_ready, 1)
                if on("C", t):
                    pool.wait_ge(v3_plain, c + 1)
                    nc.gpsimd.tensor_tensor(V3[:], V3_plain[:], B3v[:].unsqueeze(1).broadcast_to([P, 2, D]), ALU.add)\
                        .then_inc(v3_ready, 1)
                if on("P", t):
                    for i in range(2):
                        low_part(rest1, parts1, mid1, low1, i, 2 * p + i + 1)
                for j in range(N_T1):
                    if on("B", t) and j == 0:
                        root(1, ln2, N_LN2 * b + N_LN2, b)
                    if on("A", t):
                        select(t, j)
                    if on("B", t) and j == 4:
                        root(2, ln2b, N_LN2B * b + N_LN2B, b)
                if on("C", t):
                    root(3, ln3, N_LN3 * c + N_LN3, c)
                if on("C1", t):
                    for i in range(2):
                        low_part(rest3, parts3, mid3, low3, i, 2 * c1 + i + 1)
                if on("C1", t):
                    pool.wait_ge(x2_ready, 2 * c1 + 2)
                    if on("C", t):
                        pool.wait_ge(out_ready, 2 * c + 2)
                    nc.gpsimd.tensor_tensor(Y3[:], X2[:], B3o[:], ALU.add).then_inc(y3_ready, 1)
                    pool.wait_ge(y3_ready, 2 * c1 + 1)
                    nc.gpsimd.tensor_tensor(Y3[:], Y3[:], X2[:], ALU.add).then_inc(y3_ready, 1)

            steps(pool, run)

        @block.scalar
        def _(act):

            def mid_part(rest, parts, evac, n, mid, i):
                act.wait_ge(evac, n)
                nc.scalar.activation(parts[:, i, 1, :, :].rearrange("p m t -> p (m t)"), rest[:, i, :],
                                     ACT.Copy).then_inc(mid, 1)

            def norm_end(i, y, dst, seq, ready):
                act.wait_ge(rstd_ready[i], 2 * seq + 2)
                for q in range(2):
                    nc.scalar.activation(dst[:, q, :], y[:, q, :], ACT.Identity, bias=shift[:, i, q:q + 1],
                                         scale=rstd[:, i, q:q + 1]).then_inc(ready, 1)

            def biased(dst, i, fill):
                for m in range(2):
                    nc.scalar.activation(dst[:, m, :], bank_of(fill)[:, m * S:m * S + S],
                                         ACT.Identity, bias=B2[:, i, m:m + 1]).then_inc(act2, 1)

            def high_part(t, i, fill):
                act.wait_ge(proj1, 3 * t + 1 + i)
                nc.scalar.activation(parts1[:, i, 0, :, :].rearrange("p m t -> p (m t)"), bank_of(fill),
                                     ACT.Copy).then_inc(high1, 1)

            def run(t, odd):
                wait_weights(act, t)
                b = t - LAG["B"]
                if on("B", t):
                    act.wait_ge(proj2, 5 * b + 1)
                    biased(K2, 1, "K2")
                    norm_end(0, Y1, X1, b, x1_ready)
                    act.wait_ge(proj2, 5 * b + 2)
                    nc.scalar.activation(V2[:].rearrange("p m f -> p (m f)"), bank_of("V2"),
                                         ACT.Copy).then_inc(v2_ready, 1)
                    act.wait_ge(proj2, 5 * b + 3)
                    nc.scalar.activation(X1T[:].rearrange("p m t -> p (m t)"), bank_of("X1T"),
                                         ACT.Copy).then_inc(act2, 1)
                    act.wait_ge(proj2, 5 * b + 4)
                    biased(Q2, 0, "Q2")
                if on("P", t):
                    high_part(t, 0, "Pq")
                if on("B", t):
                    act.wait_ge(max2, 3 * b + 3)
                    for q, (lo, hi) in enumerate(((0, 128), (128, 384))):
                        nc.scalar.activation(P2[:].rearrange("p c k -> p (c k)")[:, lo:hi],
                                             bank_of("S2")[:, lo:hi], ACT.Exp,
                                             bias=bias2[:, q:q + 1], scale=1.0 / 16.0,
                                             accum_out=sum2[:, q:q + 1]).then_inc(act2, 1)
                if on("B", t):
                    act.wait_ge(attn2, 2 * b + 1)
                    nc.scalar.activation(PT2[:].rearrange("p c k -> p (c k)"), bank_of("PT2")[:, 0:384],
                                         ACT.Copy).then_inc(pT2, 1)
                a, c = t - LAG["A"], t - LAG["C"]
                for j in range(N_T3):
                    if on("C", t):
                        act.wait_ge(scoresT3, N_T3 * c + j + 1)
                        n = T3_COLS[j % 2]
                        nc.scalar.activation(PT3[:, j // 2, j % 2, 0:n], col_ps[:, j % 2, 0:n], ACT.Exp,
                                             scale=1.0 / 16.0).then_inc(exp3, 1)
                    if on("P", t) and j == 1:
                        high_part(t, 1, "Pk")
                    if on("P", t) and j in (1, 3):
                        mid_part(rest1, parts1, evac1, N_EV1 * t + 1 + j // 2, mid1, j // 2)
                for j in range(N_T1):
                    if on("A", t):
                        act.wait_ge(scoresT1, N_T1 * a + j + 1)
                        if j % 3 == 0:
                            wait(act, pv1, 4 * a - 1 + j // 3)
                        nc.scalar.activation(PT1[:, (j // 3) % 2, j % 3, :], col_ps[:, j % 2, :], ACT.Exp,
                                             scale=0.25).then_inc(exp1, 1)
                    if on("B", t) and j == 1:
                        norm_end(1, Y2, X2, b, x2_ready)
                    if on("B", t) and j == 6:
                        norm_end(2, X2, Z2, b, z2_ready)
                if on("C1", t):
                    c1 = t - LAG["C1"]
                    act.wait_ge(proj3, 4 * c1 + 1)
                    for rows, k, t0, t1 in NESTED:
                        nc.scalar.activation(XN[0:rows, k, t0:t1], bank_of("Z")[0:rows, k * S + t0:k * S + t1],
                                             ACT.Identity, bias=B3[0:rows, 1, k:k + 1],
                                             scale=B3[0:rows, 0, k:k + 1]).then_inc(xn_ready, 1)
                if on("C", t):
                    wait(act, out_stored, 16 * c)
                    norm_end(3, Y3, OUT, c, out_ready)
                if on("P", t):
                    act.wait_ge(proj1, 3 * t + 3)
                    if on("A", t):
                        act.wait_ge(pv1, 4 * a + 4)
                    elif fixed(t) and t == 0:
                        act.wait_ge(pool_ready, 1)
                    v = bank_of("Pv").rearrange("p (kg w u d) -> p kg w u d", kg=4, w=2, u=4)
                    dst = V1[:].rearrange("p k (g w u) e -> p (k g) w u e", g=2, w=2)
                    for w in range(2):
                        nc.scalar.activation(dst[:, :, w, :, D1 * w:D1 * w + D1], v[:, :, w, :, :],
                                             ACT.Copy).then_inc(v1_ready, 1)
                if on("C1", t):
                    for i in range(2):
                        act.wait_ge(proj3, 4 * c1 + 2 + i)
                        for m in range(2):
                            nc.scalar.activation(parts3[:, i, 0, m, :], bank_of(("C1q", "C1k")[i])[:, m * S:m * S + S],
                                                 ACT.Identity, bias=B3[:, 2 + i, m:m + 1]).then_inc(high3, 1)
                        mid_part(rest3, parts3, evac3, N_EV3 * c1 + 2 + 2 * i, mid3, i)
                    act.wait_ge(proj3, 4 * c1 + 4)
                    nc.scalar.activation(V3_plain[:].rearrange("p m f -> p (m f)"), bank_of("C1v"),
                                         ACT.Copy).then_inc(v3_plain, 1)

            steps(act, run)

        @block.vector
        def _(dve):
            dve.wait_ge(consts_in, 16)
            cst = lambda n, lo=0, hi=P: CST[lo:hi, CONST_COLS[n][0]:CONST_COLS[n][1]]
            def prepare_constants():
                nc.vector.tensor_copy(identb[:], ident).then_inc(const_ready, 1)
                for i in range(2):
                    nc.vector.tensor_copy(K1[MROW:P, i, :, :], cst("pick1", MROW, P).unsqueeze(2).broadcast_to([32, H1, S]))\
                        .then_inc(const_ready, 1)
                for i in range(2):
                    nc.vector.tensor_copy(K3[MROW:P, i, 0, :, :], cst("pick3", MROW, P).unsqueeze(2).broadcast_to([32, H3, S]))\
                        .then_inc(const_ready, 1)
                for n, blocks in MASKS.items():
                    for i, block_mask in enumerate(blocks):
                        nc.vector.tensor_copy(masks[n][:, i * P:i * P + P], cst(block_mask)).then_inc(const_ready, 1)

            def norm_stats(i, y, s):
                for q in range(2):
                    nc.vector.bn_stats(stats[:, i, q, :], y[:, q, :]).then_inc(s, 1)

            def norm_aggregate(i, s, n):
                dve.wait_ge(s, n + 2)
                nc.vector.memset(fence[:, N_SC1 + i:N_SC1 + i + 1], 0.0)
                for q in range(2):
                    nc.vector.bn_aggr(mv[:, i, q, :], stats[:, i, q, :]).then_inc(s, 1)

            def norm_moments(i, s, n):
                dve.wait_ge(s, n + 4)
                nc.vector.tensor_scalar(vare[:, i, :], mv[:, i, :, 1], EPS, None, ALU.add).then_inc(s, 1)
                nc.vector.tensor_scalar(nmean[:, i, :], mv[:, i, :, 0], -1.0, None, ALU.mult).then_inc(s, 1)

            def norm(i, y, s, base, n):
                norm_stats(i, y, s)
                norm_aggregate(i, s, base + n)
                norm_moments(i, s, base + n)

            def split_max(nmax, nmaxp, heads, maxes, n_max, split, base):
                dve.wait_ge(maxes, n_max)
                nc.vector.tensor_copy(nmaxp[:, :, 0:heads], nmax[:]).then_inc(split, 1)
                dve.wait_ge(split, base + 1)
                nc.vector.tensor_tensor(nmaxp[:, :, heads:2 * heads], nmax[:], nmaxp[:, :, 0:heads],
                                        ALU.subtract).then_inc(split, 1)

            def copy_max(mrow, fill, ready, n, copied):
                dve.wait_ge(ready, n)
                nc.vector.tensor_copy(mrow[MROW:P, :], bank_of(fill)[MROW:P, :].bitcast(BF16)[:, 0:S])\
                    .then_inc(copied, 1)

            def spread_max(mrow, dst, heads, copied, n):
                dve.wait_ge(copied, n)
                nc.vector.tensor_copy(dst, mrow[MROW:P, :].unsqueeze(1).broadcast_to([32, heads, S]))\
                    .then_inc(copied, 1)

            def row_maxima(j, heads, dst, scores, n, done):
                dve.wait_ge(scores, n)
                nc.vector.tensor_reduce(dst, row_ps[:, j % 2, :].rearrange("p (h k) -> p h k", h=heads),
                                        AX.X, ALU.max, negate=True).then_inc(done, 1)

            def masked_maxima(j, nmax, scores, n):
                dve.wait_ge(scores, n)
                nc.vector.memset(fence[:, j:j + 1], 0.0)
                for u in range(2):
                    h = 2 * (j - 4) + u
                    last = nc.vector.tensor_tensor_reduce(
                        unused[:, h, :], row_ps[:, j % 2, u * S:u * S + S], mask_last[:], -1.0, 3.0e38,
                        ALU.add, ALU.min, nmax[:, 1, h:h + 1])
                last.then_inc(max1, 1)

            def rest1_of(t, i, fill):
                dve.wait_ge(high1, 2 * t + i + 1)
                nc.vector.tensor_tensor(rest1[:, i, :], bank_of(fill), parts1[:, i, 0, :, :].rearrange(
                    "p m t -> p (m t)"), ALU.subtract).then_inc(evac1, 1)

            def rest3_of(c1, i, fill):
                dve.wait_ge(high3, 4 * c1 + 2 * i + 2)
                for m in range(2):
                    nc.vector.scalar_tensor_tensor(
                        out=rest3[:, i, m * S:m * S + S], in0=bank_of(fill)[:, m * S:m * S + S],
                        scalar=B3[:, 2 + i, m:m + 1], in1=parts3[:, i, 0, m, :],
                        op0=ALU.add, op1=ALU.subtract).then_inc(evac3, 1)

            def divide1(a, half):
                dve.wait_ge(pv1, 4 * a + 2 * half + 2)
                nc.vector.reciprocal(rsum1[:, half, :], acc[:, half, 1, :]).then_inc(norm1, 1)
                dve.wait_ge(norm1, 4 * a + 2 * half + 1)
                nc.vector.tensor_tensor(OT1[:, half, :], acc[:, half, 0, :], rsum1[:, half, :],
                                        ALU.mult).then_inc(norm1, 1)

            def run(t, odd):
                wait_weights(dve, t)
                if fixed(t) and t == 1:
                    dve.wait_ge(pool_ready, 8)
                    prepare_constants()
                a, b, c1, c = (t - LAG[x] for x in ("A", "B", "C1", "C"))
                for j in range(N_SC1):
                    if on("A", t) and j < 4:
                        row_maxima(j, 4, nmax1[:, 0, 4 * j:4 * j + 4], scores1, N_SC1 * a + j + 1, max1)
                    elif on("A", t):
                        masked_maxima(j, nmax1, scores1, N_SC1 * a + j + 1)
                    if on("B", t) and j == 0:
                        dve.wait_ge(ln1, N_LN1 * b + 2)
                        norm_stats(0, Y1, ln1)
                    if on("B", t) and j == 1:
                        norm_aggregate(0, ln1, N_LN1 * b + 2)
                    if on("B", t) and j == 2:
                        norm_moments(0, ln1, N_LN1 * b + 2)
                if on("A", t):
                    split_max(nmax1, nmaxp1, H1, max1, N_SC1 * a + N_SC1, msplit1, 2 * a)
                if on("C", t):
                    for j in range(N_SC3):
                        row_maxima(j, 2, nmax3[:, 0, 2 * j:2 * j + 2] if j < 4 else nmax3[:, 1, 0:2],
                                   scores3, N_SC3 * c + j + 1, max3)
                    split_max(nmax3, nmaxp3, H3, max3, N_SC3 * c + N_SC3, msplit3, 2 * c)
                if on("B", t):
                    dve.wait_ge(proj2, 5 * b + 5)
                    for q, (lo, hi) in enumerate(((0, 128), (128, 384))):
                        nc.vector.tensor_reduce(nmax2[:, q:q + 1], bank_of("S2")[:, lo:hi], AX.X, ALU.max,
                                                negate=True).then_inc(max2, 1)
                    dve.wait_ge(max2, 3 * b + 2)
                    nc.vector.tensor_scalar(bias2[:], nmax2[:], 1.0 / 16.0, None, ALU.mult).then_inc(max2, 1)
                if on("A", t):
                    copy_max(mrow1, "mT1", mrows1, a + 1, mcopy1)
                if on("C", t):
                    copy_max(mrow3, "mT3", mrows3, c + 1, mcopy3)
                    spread_max(mrow3, Q3[MROW:P, 1 - odd, 0, :, :], H3, mcopy3, 2 * c + 1)
                if on("P", t):
                    rest1_of(t, 0, "Pq")
                    rest1_of(t, 1, "Pk")
                if on("A", t):
                    spread_max(mrow1, Q1[MROW:P, 1 - odd, :, :], H1, mcopy1, 2 * a + 1)
                if on("B", t):
                    dve.wait_ge(act2, N_ACT2 * b + 7)
                    nc.vector.reciprocal(rsum2[:], sum2[:]).then_inc(rec2, 1)
                    dve.wait_ge(rec2, b + 1)
                    dve.wait_ge(attn2, 2 * b + 2)
                    dve.wait_ge(x1b_ready, b + 1)
                    for q in range(2):
                        nc.vector.scalar_tensor_tensor(out=Y2[:, q, :], in0=bank_of("Y2")[:, q * D:q * D + D],
                                                       scalar=rsum2[:, q:q + 1], in1=X1b[:, q, :],
                                                       op0=ALU.mult, op1=ALU.add).then_inc(ln2, 1)
                    dve.wait_ge(ln2, N_LN2 * b + 2)
                    norm(1, Y2, ln2, N_LN2 * b, 2)
                if on("C", t):
                    dve.wait_ge(pv3, c + 1)
                    for half, n in ((0, 0), (1, 6)):
                        places = [x for x in NESTED if x[1] == half]
                        for rows, k, t0, t1 in places:
                            nc.vector.reciprocal(rsum3[0:rows, k, t0:t1], acc[0:rows, k, 1, t0:t1]).then_inc(norm3, 1)
                        dve.wait_ge(norm3, 8 * c + n + len(places))
                        for rows, k, t0, t1 in places:
                            nc.vector.tensor_tensor(OT3[0:rows, k, t0:t1], acc[0:rows, k, 0, t0:t1],
                                                    rsum3[0:rows, k, t0:t1], ALU.mult).then_inc(norm3, 1)
                if on("B", t):
                    dve.wait_ge(x2_ready, 2 * b + 2)
                    norm(2, X2, ln2b, N_LN2B * b, 0)
                if on("C", t):
                    dve.wait_ge(attn3, c + 1)
                    dve.wait_ge(y3_ready, 2 * c + 2)
                    for r0, r1, tile, f0, f1 in NESTED_OUT:
                        nc.vector.tensor_tensor(Y3[r0:r1, tile, f0:f1], bank_of("C4")[r0:r1, tile * D + f0:tile * D + f1],
                                                Y3[r0:r1, tile, f0:f1], ALU.add).then_inc(ln3, 1)
                    dve.wait_ge(ln3, N_LN3 * c + 4)
                    norm(3, Y3, ln3, N_LN3 * c, 4)
                if on("A", t):
                    divide1(a, 0)
                if on("A", t):
                    divide1(a, 1)
                if on("C1", t):
                    rest3_of(c1, 0, "C1q")
                if on("C1", t):
                    rest3_of(c1, 1, "C1k")
                if on("A", t):
                    dve.wait_ge(attn1, a + 1)
                    dve.wait_ge(x_in, 16 * a + 16)
                    for q in range(2):
                        nc.vector.tensor_tensor(Y1[:, q, :], bank_of("A4")[:, q * D:q * D + D], XR[:, q, :],
                                                ALU.add).then_inc(ln1, 1)

            steps(dve, run)

        @block.tensor
        def _(pe):
            mm = nc.tensor.matmul

            def tokens_by_feature(fill, w, xt, i, cols=S):
                m, k = i // 2, i % 2
                n = S if k == 0 else cols
                return mm(bank_of(fill)[:, m * S:m * S + n], w[:, k, m * P:m * P + P], xt[:, k, 0:n],
                          start=(k == 0), stop=(k == 1), skip_group_check=True)

            def features_by_token(fill, w, xt, q):
                for k in range(2):
                    last = mm(bank_of(fill)[:, q * D:q * D + D], xt[:, k, q * P:q * P + P], w[:, k, 0:D],
                              start=(k == 0), stop=(k == 1))
                return last

            def turn(fill, src):
                for k in range(2):
                    for q in range(2):
                        last = nc.tensor.transpose(bank_of(fill)[:, k * S + q * P:k * S + q * P + P],
                                                   src[:, q, k * P:k * P + P], ident)
                return last

            def project(t, fill, ready, n, w, xt, i, done):
                if i == 0:
                    pe.wait_ge(ready, n)
                    bank_free(pe, t, fill)
                last = tokens_by_feature(fill, w, xt, i)
                if i == 3:
                    last.then_inc(done, 1)

            def Z(t):
                c = t - LAG["C1"]
                pe.wait_ge(z2_ready, 2 * c + 2)
                bank_free(pe, t, "Z")
                turn("Z", Z2).then_inc(proj3, 1)

            def C1_qk(t):
                c = t - LAG["C1"]
                pe.wait_ge(xn_ready, 4 * c + 4)
                for fill, w in (("C1q", W3q), ("C1k", W3k)):
                    bank_free(pe, t, fill)
                    for i in range(4):
                        last = tokens_by_feature(fill, w, XN, i, P)
                    last.then_inc(proj3, 1)

            def C1_v(t):
                bank_free(pe, t, "C1v")
                bank = bank_of("C1v")
                mm(bank[:, 0:D], XN[:, 0, 0:P], W3v[:, 0, :], start=True, stop=False)
                mm(bank[:, 0:D], XN[:, 1, 0:P], W3v[:, 1, :], start=False, stop=True)
                mm(bank[:, D:2 * D], XN[:, 0, P:S], W3v[:, 0, :], start=True, stop=True).then_inc(proj3, 1)

            def A2_scores(t, j, q1, k1):
                a = t - LAG["A"]
                bank = row_ps[:, j % 2, :]
                if j == 0:
                    pe.wait_ge(stacks1_in, 192 * a + 192)
                if j >= 2:
                    pe.wait_ge(max1, N_SC1 * a + j - 1)
                else:
                    bank_free(pe, t, ("A2_0", "A2_1")[j])
                if j < 4:
                    mm(bank, identb[:], masks["mask_q0"][:], start=True, stop=False)
                    for u in range(4):
                        h = 4 * j + u
                        last = mm(bank[:, u * P:u * P + P], q1[0:MROW, h, 0:P], k1[0:MROW, h, 0:P],
                                  start=False, stop=(u == 3))
                else:
                    for u in range(2):
                        h = 2 * (j - 4) + u
                        last = mm(bank[:, u * S:u * S + S], q1[0:MROW, h, P:S], k1[0:MROW, h, :],
                                  start=True, stop=True)
                last.then_inc(scores1, 1)

            def C2_scores(t, j, q3, k3):
                c = t - LAG["C"]
                if j == 0:
                    pe.wait_ge(stacks3_in, 192 * c + 192)
                if j >= 2:
                    pe.wait_ge(max3, N_SC3 * c + j - 1)
                else:
                    bank_free(pe, t, ("C2_0", "C2_1")[j])
                q, h0 = (0, 2 * j) if j < 4 else (1, 0)
                for u in range(2):
                    for s in range(2):
                        last = mm(row_ps[:, j % 2, u * S:u * S + S], q3[0:MROW, s, h0 + u, q * P:q * P + P],
                                  k3[0:MROW, s, h0 + u, :], start=(s == 0), stop=(s == 1))
                last.then_inc(scores3, 1)

            def turn_max(t, stage, fill, split, nmaxp, ready):
                bank_free(pe, t, fill)
                pe.wait_ge(split, 2 * (t - LAG[stage]) + 2)
                rows = bank_of(fill)[MROW:P, :].bitcast(BF16)
                for q in range(2):
                    last = nc.tensor.transpose(rows[:, q * P:q * P + P], nmaxp[:, q, :], identb[:])
                last.then_inc(ready, 1)

            def turn_X1(t):
                pe.wait_ge(x1_ready, 2 * (t - LAG["B"]) + 2)
                bank_free(pe, t, "X1T")
                turn("X1T", X1).then_inc(proj2, 1)

            def S2(t):
                pe.wait_ge(act2, N_ACT2 * (t - LAG["B"]) + 5)
                bank_free(pe, t, "S2")
                bank = bank_of("S2")
                mm(bank[:, 0:P], identb[:], masks["mask_q0"][:, 0:P], start=True, stop=False)
                for k in range(2):
                    mm(bank[:, 0:P], Q2[:, k, 0:P], K2[:, k, 0:P], start=False, stop=(k == 1))
                mm(bank[:, S:S + P], identb[:], masks["mask_q0"][:, 0:P], start=True, stop=False,
                   skip_group_check=True)
                for k in range(2):
                    last = mm(bank[:, P:P + S], Q2[:, k, P:S], K2[:, k, :], start=False, stop=(k == 1),
                              skip_group_check=True)
                last.then_inc(proj2, 1)

            def V2_projection(t, q):
                if q == 0:
                    bank_free(pe, t, "V2")
                last = features_by_token("V2", W2v, CT, q)
                if q == 1:
                    last.then_inc(proj2, 1)

            def turn_P2(t):
                pe.wait_ge(act2, N_ACT2 * (t - LAG["B"]) + 7)
                bank_free(pe, t, "PT2")
                for i in range(3):
                    last = nc.tensor.transpose(bank_of("PT2")[:, i * P:i * P + P], P2[:, i, :], ident)
                last.then_inc(attn2, 1)

            def Y2_product(t):
                b = t - LAG["B"]
                pe.wait_ge(pT2, b + 1)
                pe.wait_ge(v2_ready, b + 1)
                bank_free(pe, t, "Y2")
                bank = bank_of("Y2")
                mm(bank[:, 0:D], PT2[:, 0, :], V2[:, 0, :], start=True, stop=True)
                mm(bank[:, D:2 * D], PT2[:, 1, :], V2[:, 0, :], start=True, stop=False)
                mm(bank[:, D:2 * D], PT2[:, 2, :], V2[:, 1, :], start=False, stop=True).then_inc(attn2, 1)

            def C3_scores(t, j, q3, k3):
                c = t - LAG["C"]
                if j == 0:
                    pe.wait_ge(mcopy3, 2 * c + 2)
                if j >= 2:
                    pe.wait_ge(exp3, N_T3 * c + j - 1)
                elif fixed(c):
                    pe.wait_ge(exp1, N_T1 * min(t - LAG["A"], NB))
                    wait(pe, exp3, N_T3 * c)
                else:
                    pe.wait_ge(exp1, N_T1 * (t - LAG["A"]))
                keys = slice((j // 2) * P, (j // 2) * P + P)
                for h, col in T3_BANKS[j % 2]:
                    n = Q3_USED[h]
                    for s, rows_used in ((0, P), (1, MROW)):
                        last = mm(col_ps[:, j % 2, col:col + n], k3[0:rows_used, s, h, keys],
                                  q3[0:rows_used, s, h, 0:n], start=(s == 0), stop=(s == 1))
                last.then_inc(scoresT3, 1)

            def C3_products(t):
                c = t - LAG["C"]
                if fixed(c):
                    pe.wait_ge(norm1, 4 * min(t - LAG["A"], NB))
                    wait(pe, norm3, 8 * c)
                else:
                    pe.wait_ge(norm1, 4 * (t - LAG["A"]))
                pe.wait_ge(v3_ready, c + 1)
                place = {h: (f, col) for f in range(2) for h, col in T3_BANKS[f]}
                for k in range(2):
                    pe.wait_ge(exp3, N_T3 * c + 2 * k + 2)
                    for half in range(2):
                        for i in range(2):
                            for u in range(4):
                                h = 4 * half + u
                                f, col = place[h]
                                n = Q3_USED[h]
                                w = V3[:, k, D3 * h:D3 * h + D3] if i == 0 else ones32[:]
                                last = mm(acc[32 * u:32 * u + 32, half, i, 0:n], w, PT3[:, k, f, col:col + n],
                                          start=(k == 0 and i == 0), stop=(k == 1), skip_group_check=True)
                last.then_inc(pv3, 1)

            def A3_scores(t, g, f, q1, k1):
                a = t - LAG["A"]
                j = 3 * g + f
                bank = col_ps[:, j % 2, :]
                if j == 0:
                    pe.wait_ge(mcopy1, 2 * a + 2)
                if j >= 2:
                    pe.wait_ge(exp1, N_T1 * a + j - 1)
                else:
                    if not fixed(t) or t >= LAG["C"]:
                        pe.wait_ge(exp3, N_T3 * (t - LAG["C"] + 1))
                    if fixed(a):
                        wait(pe, exp1, N_T1 * a)
                if f < 2:
                    for u in range(2):
                        h = 4 * g + 2 * f + u
                        mm(bank[:, u * S:u * S + S], k1[:, h, 0:P], q1[:, h, :], start=(u == 0), stop=False,
                           skip_group_check=True)
                    last = mm(bank.rearrange("p (u w q) -> p u w q", u=2, w=2)[:, :, 1, :], identb[:],
                              masks["mask_k0"][:].rearrange("p (u q) -> p u q", u=2), start=False, stop=True,
                              skip_group_check=True)
                else:
                    for u in range(4):
                        h = 4 * g + u
                        last = mm(bank[:, u * P:u * P + P], k1[:, h, P:S], q1[:, h, P:S], start=True, stop=True)
                last.then_inc(scoresT1, 1)

            def A3_products(t, g, f):
                a = t - LAG["A"]
                p = PT1[:, g % 2, :, :]
                even = g % 2 == 0
                ones = ones_lo if even else ones_hi
                bank = acc[:, g // 2, :, :]
                if g == 0 and f == 0:
                    pe.wait_ge(v1_ready, 2 * a + 2)
                    if fixed(a):
                        wait(pe, norm1, 4 * a)
                if g % 2 == 0 and f == 0 and (not fixed(t) or t >= LAG["C"]):
                    pe.wait_ge(norm3, 8 * (t - LAG["C"]) + (6 if g == 0 else 8))
                if f < 2:
                    pe.wait_ge(select1, N_T1 * a + 3 * g + 2)
                    for u in range(4):
                        w = V1[:, 0, 4 * g + u, :] if f == 0 else ones
                        mm(bank[32 * u:32 * u + 32, f, :], w, p[:, u // 2, (u % 2) * S:(u % 2) * S + S],
                           start=(even and f == 0), stop=False, skip_group_check=True)
                else:
                    pe.wait_ge(select1, N_T1 * a + 3 * g + 3)
                    for i in range(2):
                        for u in range(4):
                            w = V1[:, 1, 4 * g + u, :] if i == 0 else ones
                            last = mm(bank[32 * u:32 * u + 32, i, P:S], w, p[:, 2, u * P:u * P + P],
                                      start=False, stop=not even, skip_group_check=True)
                    last.then_inc(pv1, 1)

            def P_v(t):
                if fixed(t) and t == 0:
                    pe.wait_ge(w1v_in, 16)
                bank_free(pe, t, "Pv")
                features_by_token("Pv", W1[:, :, 2 * D:3 * D], XT, 0)
                features_by_token("Pv", W1[:, :, 2 * D:3 * D], XT, 1).then_inc(proj1, 1)

            def A4(t):
                pe.wait_ge(norm1, 4 * (t - LAG["A"]) + 4)
                bank_free(pe, t, "A4")
                features_by_token("A4", W1o, OT1, 0)
                features_by_token("A4", W1o, OT1, 1).then_inc(attn1, 1)

            def C4(t):
                pe.wait_ge(norm3, 8 * (t - LAG["C"]) + 8)
                bank_free(pe, t, "C4")
                bank = bank_of("C4")
                mm(bank[:, 0:D], OT3[:, 0, 0:P], W3o[:, 0, :], start=True, stop=False)
                mm(bank[:, 0:D], OT3[:, 1, 0:P], W3o[:, 1, :], start=False, stop=True)
                mm(bank[:, D:D + P], OT3[:, 0, P:S], W3o[:, 0, 0:P], start=True, stop=True).then_inc(attn3, 1)

            def run(t, odd):
                b = t - LAG["B"]
                wait_weights(pe, t)
                if fixed(t) and t == 1:
                    pe.wait_ge(const_ready, 11)
                    pe.wait_ge(pool_ready, 8)
                K2_PLACES = {1: (0, 1), 2: (2,), 3: (3,)}
                q1, k1 = Q1[:, 1 - odd], K1[:, 1 - odd]
                q3, k3 = Q3[:, 1 - odd], K3[:, 1 - odd]
                for j in range(N_SC1):
                    if on("A", t):
                        A2_scores(t, j, q1, k1)
                    if on("B", t) and j in K2_PLACES:
                        for i in K2_PLACES[j]:
                            project(t, "K2", ctxT_in, 16 * b + 16, W2k, CT, i, proj2)
                    if on("B", t) and j in (4, 6):
                        V2_projection(t, (j - 4) // 2)
                    if on("B", t) and j == 8:
                        turn_X1(t)
                    if on("P", t) and j >= 9:
                        project(t, "Pq", xT_in, 16 * t + 16, W1[:, :, 0:D], XT, j - 9, proj1)
                    if on("B", t) and j >= 10:
                        project(t, "Q2", act2, N_ACT2 * b + 3, W2q, X1T, j - 10, proj2)
                for j in range(N_SC3):
                    if on("C", t):
                        C2_scores(t, j, q3, k3)
                    if on("B", t) and j < 2:
                        project(t, "Q2", act2, N_ACT2 * b + 3, W2q, X1T, j + 2, proj2)
                    if on("P", t) and j == 2:
                        project(t, "Pq", xT_in, 16 * t + 16, W1[:, :, 0:D], XT, 3, proj1)
                if on("B", t):
                    S2(t)
                if on("A", t):
                    turn_max(t, "A", "mT1", msplit1, nmaxp1, mrows1)
                if on("P", t):
                    for i in range(2):
                        project(t, "Pk", xT_in, 16 * t + 16, W1[:, :, D:2 * D], XT, i, proj1)
                if on("C", t):
                    turn_max(t, "C", "mT3", msplit3, nmaxp3, mrows3)
                if on("P", t):
                    project(t, "Pk", xT_in, 16 * t + 16, W1[:, :, D:2 * D], XT, 2, proj1)
                if on("B", t):
                    turn_P2(t)
                for j in range(N_T3):
                    if on("C", t):
                        C3_scores(t, j, q3, k3)
                    if on("P", t) and j == 1:
                        project(t, "Pk", xT_in, 16 * t + 16, W1[:, :, D:2 * D], XT, 3, proj1)
                    if on("B", t) and j == 2:
                        Y2_product(t)
                if on("C", t):
                    C3_products(t)
                for g in range(5):
                    for f in range(3):
                        if on("A", t) and g < 4:
                            A3_scores(t, g, f, q1, k1)
                        if on("P", t) and (g, f) == (0, 1):
                            P_v(t)
                        if on("C", t) and (g, f) == (2, 0):
                            C4(t)
                        if on("C1", t) and (g, f) == (4, 0):
                            Z(t)
                        if on("A", t) and g > 0:
                            A3_products(t, g - 1, f)
                if on("C1", t):
                    C1_qk(t)
                if on("A", t):
                    A4(t)
                if on("C1", t):
                    C1_v(t)

            pe.wait_ge(w1_in, 16)
            steps(pe, run)


def layer_constants():
    import numpy as np
    c = np.zeros((P, CONST_W), np.float32)

    def put(name, a, rows=slice(None)):
        c[rows, CONST_COLS[name][0]:CONST_COLS[name][1]] = a

    i, j = np.arange(P)[:, None], np.arange(P)[None, :]
    causal = np.where(j <= i, 0.0, NEG)
    band = np.where((j > i) | (j < PREFIX), 0.0, NEG)
    put("ident", np.eye(P))
    put("causal", causal)
    put("band", band)
    put("bandT", band.T)
    ones = np.zeros((P, 64))
    ones[:, 0:D1] = 1.0
    ones[:, 32 + D1:64] = 1.0
    put("ones", ones)
    for name, heads in (("pick1", H1), ("pick3", H3)):
        pick = np.zeros((32, heads))
        for h in range(heads):
            pick[[h, heads + h], h] = 1.0
        put(name, pick, slice(MROW, P))
    return c


def kernel(**inputs):
    import numpy as np
    import concourse.bacc as bacc
    from concourse.bass_utils import run_bass_kernel_spmd

    g = {k: np.asarray(v) for k, v in inputs.items()}
    nc = bacc.Bacc("TRN2", target_bir_lowering=False, num_devices=1)

    def by_feature(a):
        return a.reshape(NB * S, 2, P).transpose(2, 1, 0)

    def by_token(a):
        return a.reshape(NB * 2, P, D).transpose(1, 0, 2)

    def halves(*vs):
        return np.stack([v.reshape(2, P) for v in vs]).transpose(2, 0, 1)

    w_out = g["L0_attn_w_out"].T.reshape(2, 2, 4, D1, D).transpose(0, 2, 1, 3, 4).reshape(D, D)
    arrays = {
        "xT": by_feature(g["x"]), "x": by_token(g["x"]), "ctxT": by_feature(g["ctx_1024"]),
        "consts": layer_constants(),
        "w1_qkvT": g["L0_attn_w_qkv"].T, "w1_oT": w_out,
        "w2_qT": g["L0_xattn_wq_w"].T, "w2_kT": g["L0_xattn_wk_w"].T, "w2_vT": g["L0_xattn_wv_w"].T,
        "b2": halves(g["L0_xattn_wq_b"], g["L0_xattn_wk_b"]), "bv2": g["L0_xattn_wv_b"],
        "w3_qT": g["L0_ffn_q_w"].T, "w3_kT": g["L0_ffn_k_w"].T, "w3_vT": g["L0_ffn_v_w"].T,
        "w3_oT": g["L0_ffn_o_w"].T,
        "b3": halves(g["L0_ffn_norm_w"], g["L0_ffn_norm_b"], g["L0_ffn_q_b"], g["L0_ffn_k_b"]),
        "bv3": g["L0_ffn_v_b"], "bo3": g["L0_ffn_o_b"],
    }
    arrays = {k: np.ascontiguousarray(v) for k, v in arrays.items()}
    args = [nc.dram_tensor(f"in_{k}", v.shape, mybir.dt.from_np(v.dtype), kind="ExternalInput").ap()
            for k, v in arrays.items()]
    out = nc.dram_tensor("out", (P, NB * 2, D), F32, kind="ExternalOutput").ap()
    build(nc, *args, out)
    r = run_bass_kernel_spmd(nc, [{f"in_{k}": v for k, v in arrays.items()}], core_ids=[0])
    got = np.asarray(r.results[0]["out"])
    return got.transpose(1, 0, 2).reshape(NB, S, D)
```
